# Optimizing a Trainium2 kernel written in Bass

```python
import numpy as np
import jax
import jax.numpy as jnp

def _softmax(x, axis=-1):
    return jax.nn.softmax(x, axis=axis)

def _gelu(x):
    return jax.nn.gelu(x, approximate=True)

def _silu(x):
    return jax.nn.silu(x)

def _sigmoid(x):
    return jax.nn.sigmoid(x)

def _layernorm(x, axis=-1, eps=1e-05):
    m = jnp.mean(x, axis=axis, keepdims=True)
    v = jnp.var(x, axis=axis, keepdims=True)
    return (x - m) / jnp.sqrt(v + eps)

def _scatter_add(tgt, idx, src, axis=0):
    return tgt.at[idx].add(src)

def _segment_sum(src, seg, n):
    return jax.ops.segment_sum(src, seg, n)
kernel_name = 'mk_gnn_preln_d1_gnn_r8_851e41'

def setup_inputs(seed: int=0):
    np.random.seed(seed)
    _w = jnp.asarray

    def _rec_inputs():
        import jax
        import jax.numpy as jnp
        _gk = jax.random.key(seed)
        x = -0.000202 + 1 * jax.random.normal(jax.random.fold_in(_gk, 1), (12500, 128), jnp.float32)
        src = jax.random.randint(jax.random.fold_in(_gk, 2), (200000,), 0, 12500, jnp.int32)
        dst = jnp.minimum((12500 * jax.random.uniform(jax.random.fold_in(_gk, 3), (200000,)) ** 2.0).astype(jnp.int32), 99999)
        _o = jnp.argsort(dst, stable=True)
        src = src[_o]
        dst = dst[_o]
        edge_attr_64 = 0.000155561 + 1.00019 * jax.random.normal(jax.random.fold_in(_gk, 11), (200000, 64), jnp.float32)
        return (x, src, dst, edge_attr_64)
    x, src, dst, edge_attr_64 = _rec_inputs()

    def _L0_gnn_setup():
        import jax, jax.numpy as jnp
        import numpy as np
        N_NODES, N_EDGES = (6250, 75000)
        NODE_DIM, EDGE_DIM = (128, 64)
        H, HD = (4, 32)
        key = jax.random.key(seed)
        k = jax.random.split(key, 6)
        node_features = jax.random.normal(k[0], (N_NODES, NODE_DIM), jnp.float32)
        edge_indices = jax.random.randint(k[1], (2, N_EDGES), 0, N_NODES, jnp.int32)
        edge_features = jax.random.normal(k[2], (N_EDGES, EDGE_DIM), jnp.float32)
        W_node = jax.random.normal(k[3], (H * HD, NODE_DIM), jnp.float32) / np.sqrt(NODE_DIM).astype(np.float32)
        W_edge = jax.random.normal(k[4], (H * HD, EDGE_DIM), jnp.float32) / np.sqrt(EDGE_DIM).astype(np.float32)
        a = jax.random.normal(k[5], (H, 3 * HD), jnp.float32)
        return {'node_features': node_features, 'edge_indices': edge_indices, 'edge_features': edge_features, 'W_node': W_node, 'W_edge': W_edge, 'a': a}
    _L0_gnn_all = _L0_gnn_setup()
    _L0_gnn_in = {k: v for k, v in _L0_gnn_all.items() if k in ('W_node', 'W_edge', 'a')}
    del _L0_gnn_all
    return {'x': x, 'src': src, 'dst': dst, 'edge_attr_64': edge_attr_64, 'L0_gnn_W_node': _L0_gnn_in['W_node'], 'L0_gnn_W_edge': _L0_gnn_in['W_edge'], 'L0_gnn_a': _L0_gnn_in['a']}

def reference(x, src, dst, edge_attr_64, L0_gnn_W_node, L0_gnn_W_edge, L0_gnn_a):
    import jax
    import jax.numpy as jnp

    def _L0_gnn_ref(node_features, edge_indices, edge_features, W_node, W_edge, a):
        import jax, jax.numpy as jnp
        import numpy as np
        N_NODES, N_EDGES = (6250, 75000)
        NODE_DIM, EDGE_DIM = (128, 64)
        H, HD = (4, 32)
        num_nodes = node_features.shape[0]
        num_edges = edge_indices.shape[1]
        h = (node_features @ W_node.T).reshape(num_nodes, H, HD)
        e = (edge_features @ W_edge.T).reshape(num_edges, H, HD)
        src, tgt = (edge_indices[0], edge_indices[1])
        h_src = h[src]
        h_tgt = h[tgt]
        att_in = jnp.concatenate([h_src, h_tgt, e], axis=-1)
        att = jnp.sum(att_in * a, axis=-1)
        att = jnp.where(att > 0, att, 0.2 * att)
        m = jnp.maximum(jax.ops.segment_max(att, tgt, num_segments=num_nodes), 0.0)
        ex = jnp.exp(att - m[tgt])
        ones = jnp.ones((num_edges,), node_features.dtype)
        deg = jax.ops.segment_sum(ones, tgt, num_segments=num_nodes)
        denom = jax.ops.segment_sum(ex, tgt, num_segments=num_nodes) + (num_edges - deg)[:, None] * jnp.exp(-m)
        w = ex / denom[tgt]
        h_prime = jax.ops.segment_sum(w[:, :, None] * h_src, tgt, num_segments=num_nodes)
        return h_prime.reshape(num_nodes, H * HD)
    edge_index = jnp.stack([src, dst])
    h = jnp.maximum(_layernorm(x, axis=-1), 0.0)
    x = x + _L0_gnn_ref(h, edge_index, edge_attr_64, L0_gnn_W_node, L0_gnn_W_edge, L0_gnn_a)
    return x

_drawn_inputs = setup_inputs


def setup_inputs(seed=0):
    import zlib

    import numpy as np

    out = dict(_drawn_inputs(seed))
    spreads = {}
    factors = {}
    for name, (base, spread) in spreads.items():
        noise = np.random.default_rng([zlib.crc32(name.encode()), seed]).standard_normal(out[name].shape)
        drawn = base * np.exp(spread * noise) if base else spread * noise
        out[name] = jnp.asarray(drawn.astype(out[name].dtype))
    for name, factor in factors.items():
        out[name] = (out[name] * factor).astype(out[name].dtype)
    return out
```

```python
import concourse.bass as bass
from concourse import mybir
from contextlib import ExitStack

N_NODES, N_EDGES, NODE_DIM, EDGE_DIM = 12500, 200000, 128, 64
HEADS, HD = 4, 32
P = 128
N_BLOCKS = -(-N_NODES // P)
N_TILES = -(-N_EDGES // P)
TB = -(-(N_TILES + N_BLOCKS - 1) // P)
NS = TB * P
GS = 16
NG = NS // GS
HS = HEADS * GS
ROW = NODE_DIM + HEADS
HC = HD + 1
ACC = HEADS * HC
PAD_DST = 1 << 20
NODE_GROUP = 7
N_NODE_GROUPS = N_BLOCKS // NODE_GROUP
EPS = 1e-5


def gat_kernel(nc, x, src, dst, ea, w_node, w_edge, a, out):
    f32, bf16, i32 = mybir.dt.float32, mybir.dt.bfloat16, mybir.dt.int32
    ALU = mybir.AluOpType
    ACT = mybir.ActivationFunctionType
    X = mybir.AxisListType.X
    ds = bass.ds

    table = nc.dram_tensor("node_table", [N_BLOCKS * P, ROW], f32, kind="Internal").ap()

    ctx = ExitStack()
    with ctx:
        def sb(name, shape, dt):
            return ctx.enter_context(nc.sbuf_tensor(name, shape, dt))

        def pb(name, shape, dt=f32):
            return ctx.enter_context(nc.psum_tensor(name, shape, dt))

        def sem(name):
            return ctx.enter_context(nc.semaphore(name))

        acc = sb("acc", [P, (N_BLOCKS + 1) * ACC], f32)
        acc_b = acc[:, :].rearrange("p (b c) -> p b c", c=ACC)
        gath = sb("gath", [P, 2, GS, ROW], f32)
        vals = sb("vals", [P, GS, ACC], f32)
        onehot = sb("onehot", [P, 2, GS, P], f32)
        onehot_b = sb("onehot_b", [P, GS, P], bf16)
        onehot_t = sb("onehot_t", [P, GS, P], bf16)
        eattr = sb("eattr", [P, 2, GS, EDGE_DIM], f32)
        eattr_t = sb("eattr_t", [P, 2, 4 * P], f32)
        idx = sb("idx", [P, 2, GS], i32)
        src_s = sb("src_s", [P, NS], f32)
        rel_s = sb("rel_s", [P, NS], f32)
        last_s = sb("last_s", [P, NS], f32)
        block_1h = sb("block_1h", [P, NS], bf16)
        first_ind = sb("first_ind", [P, NG], f32)
        eq_row = sb("eq_row", [1, NS], bf16)
        thru_row = sb("thru_row", [1, NS], bf16)
        block_row = sb("block_row", [1, NS], i32)
        start_row = sb("start_row", [1, NS], i32)
        ident = sb("ident", [P, P], f32)
        ident_b = sb("ident_b", [P, P], bf16)
        iota = sb("iota", [P, 2 * P], f32)
        pcol = sb("pcol", [P, 1], f32)
        ones = sb("ones", [1, P], f32)
        w_proj = sb("w_proj", [P, NODE_DIM + 2 * HEADS], f32)
        w_eatt = sb("w_eatt", [P, 2 * HEADS], f32)
        a_mat = sb("a_mat", [P, 3 * HEADS], f32)
        wn = sb("wn", [P, NODE_DIM], f32)
        we2 = sb("we2", [P, 2, EDGE_DIM], f32)
        tgt = sb("tgt", [P, N_BLOCKS, HEADS], f32)
        tgt_parts = sb("tgt_parts", [P, 3, N_BLOCKS, HEADS], bf16)
        tgt_t = sb("tgt_t", [P, 3 * HEADS, P], bf16)
        tgt_slot = sb("tgt_slot", [P, 3 * HEADS, GS], bf16)
        relg = sb("relg", [P, HEADS, GS], f32)
        u = sb("u", [P, HEADS, GS], f32)
        z = sb("z", [P, HEADS, GS], f32)
        att = sb("att", [P, HEADS, GS], f32)
        arg = sb("arg", [P, HEADS, GS], f32)
        ex = sb("ex", [P, HEADS, GS], f32)
        enm = sb("enm", [P, HEADS, GS], f32)
        lastex = sb("lastex", [P, HEADS, GS], f32)
        att_r = sb("att_r", [HS, P], f32)
        rel_r = sb("rel_r", [HS, P], f32)
        same = sb("same", [HS, P + 1], f32)
        fmax = sb("fmax", [HS, P], f32)
        rmax = sb("rmax", [HS, P], f32)
        from_first = sb("from_first", [HS, P], f32)
        from_last = sb("from_last", [HS, P], f32)
        rm1 = sb("rm1", [HS, P], f32)
        mx = sb("mx", [HS, P], f32)
        thru = sb("thru", [1, HEADS * (GS + 1) + 1], f32)
        lmax = sb("lmax", [1, HEADS, GS + 1], f32)
        mfwd = sb("mfwd", [1, HEADS * (GS + 1)], f32)
        fcont = sb("fcont", [1, HEADS, GS + 1], f32)
        mbase = sb("mbase", [1, HEADS * (GS + 1)], f32)
        mrun = sb("mrun", [1, HEADS, GS + 1], f32)
        cfirst = sb("cfirst", [1, HEADS, GS], f32)
        clast = sb("clast", [1, HEADS, GS], f32)
        drop = sb("drop", [1, HEADS], f32)
        alpha_arg = sb("alpha_arg", [P, HEADS], f32)
        alpha = sb("alpha", [P, HEADS], f32)

        bank = [pb(f"bank{i}", [P, 512]) for i in range(6)]
        ps_oht = pb("ps_oht", [P, GS, P], bf16)

        def v3(t, cols):
            return t.rearrange("p (a c) -> p a c", c=cols)

        def tmp(n):
            off = [0]
            for m in (NS,) * 5 + (2 * P * TB,):
                off.append(off[-1] + m)
            return acc[:, off[n]:off[n + 1]]

        t_dst, t_a, t_b, t_c, t_last = tmp(0), tmp(1), tmp(2), tmp(3), tmp(4)
        sel = tmp(5).rearrange("p (k s) -> p k s", k=TB)
        t_src = gath[:, :, :, :].rearrange("p a s r -> p (a s r)")[:, 0:NS]
        gidx = gath[:, :, :, :].rearrange("p a s r -> p (a s r)")[:, NS:2 * NS]
        oh_flat = onehot[:, :, :, :].rearrange("p a s r -> p (a s r)")
        i_dst = oh_flat[:, 0:NS].bitcast(i32)
        i_other = oh_flat[:, NS:2 * NS].bitcast(i32)
        i_src = vals[:, :, :].rearrange("p s c -> p (s c)")[:, 0:NS].bitcast(i32)
        t_hi = onehot_b[:, :, :].rearrange("p s c -> p (s c)").bitcast(f32)
        i_iota = eattr_t[:, 0, 0:2 * P].bitcast(i32)
        reset = src_s
        i_firstkey, i_lastkey = oh_flat[:, 0:NS], oh_flat[:, NS:2 * NS]

        with ExitStack() as stage:
            def ssem(name):
                return stage.enter_context(nc.semaphore(name))

            def ssb(name, shape, dt):
                return stage.enter_context(nc.sbuf_tensor(name, shape, dt))

            small = ssb("small", [P, 16, TB], f32)
            bmin, bmax, cnt, before, end, base, tile_no, kfirst = (small[:, i, :] for i in range(8))
            s1, s2 = small[:, 8, :], small[:, 9, :]
            row = ssb("row", [1, NS + 1], f32)
            rowscan = ssb("rowscan", [1, NS + 1], f32)
            slot_no = ssb("slot_no", [P, NS], f32)
            block_s = ssb("block_s", [P, NS], f32)

            s_w, s_ints, s_amat0, s_a = ssem("weights_loaded"), ssem("ints_loaded"), ssem("a_zeroed"), ssem("a_loaded")
            s_prev, s_next, s_prev_free = ssem("prev_loaded"), ssem("next_loaded"), ssem("other_ints_free")
            s_id, s_id0, s_iota, s_iota_free = ssem("ident_made"), ssem("ident_zeroed"), ssem("iota_made"), ssem("iota_free")
            s_dve, s_act = ssem("dve_step"), ssem("act_step")
            s_wt_ps, s_tp, s_colps, s_selps = ssem("weights_projected"), ssem("rows_transposed"), ssem("columns_back"), ssem("slots_selected")
            s_rowsrc, s_row, s_rowfree, s_sel, s_selfree = ssem("row_source"), ssem("row_scanned"), ssem("row_bank_free"), ssem("sel_made"), ssem("sel_bank_free")

            def tiles(n):
                return dst[n:n + NS * P].rearrange("(k q p) -> q k p", q=P, p=P)

            with nc.Block() as block:
                @block.sync
                def _(sp):
                    sp.dma_start(v3(i_dst, P), tiles(1)).then_inc(s_ints, 16)
                    sp.dma_start(v3(i_src, P), src.rearrange("(k q p) -> q k p", q=P, p=P)).then_inc(s_ints, 16)
                    sp.dma_start(v3(i_other, P), tiles(0)).then_inc(s_prev, 16)
                    sp.dma_start(wn[:, :], w_node).then_inc(s_w, 16)
                    for j in range(2):
                        sp.dma_start(we2[:, j, :], w_edge).then_inc(s_w, 16)
                    sp.wait_ge(s_amat0, 1)
                    for h in range(HEADS):
                        sp.dma_start(a_mat[h * HD:(h + 1) * HD, h:3 * HEADS:HEADS],
                                     a[h, :].rearrange("(s d) -> d s", s=3),
                                     allow_slow_non_contiguous=True).then_inc(s_a, 16)
                    sp.wait_ge(s_prev_free, 1)
                    sp.dma_start(v3(i_other, P), tiles(2)).then_inc(s_next, 16)

                @block.gpsimd
                def _(pool):
                    pool.memset(ident[:, :], 0.0).then_inc(s_id0, 1)
                    pool.wait_ge(s_id0, 1)
                    pool.affine_select(out=ident[:, :], in_=ident[:, :], compare_op=ALU.not_equal, fill=1.0,
                                       base=0, pattern=[[-1, P]], channel_multiplier=1).then_inc(s_id, 1)
                    for n, (view, pattern, base_, mult) in enumerate((
                            (i_iota, [[1, 2 * P]], 0, 0), (i_iota[:, 0:1], [[1, 1]], 0, 1),
                            (i_iota[:, 0:TB], [[P, TB]], 0, 1), (i_iota[:, 0:TB], [[P, TB]], 0, 0))):
                        if n:
                            pool.wait_ge(s_iota_free, n)
                        pool.iota(view, pattern=pattern, base=base_, channel_multiplier=mult).then_inc(s_iota, 1)
                    pool.wait_ge(s_iota_free, 4)
                    pool.iota(block_s[:, :].bitcast(i32), pattern=[[1, NS]], base=0, channel_multiplier=0).then_inc(s_iota, 1)
                    pool.wait_ge(s_iota_free, 5)
                    pool.iota(v3(block_s[:, :].bitcast(i32), P), pattern=[[P * P, TB], [1, P]], base=0,
                              channel_multiplier=P).then_inc(s_iota, 1)

                @block.vector
                def _(dve):
                    step = [0]

                    def link(ins):
                        step[0] += 1
                        ins.then_inc(s_dve, 1)
                        dve.wait_ge(s_dve, step[0])

                    V = nc.vector
                    V.memset(a_mat[:, :], 0.0).then_inc(s_amat0, 1)
                    link(V.memset(reset[:, :], 1.0))
                    link(V.memset(v3(reset[:, :], P)[:, :, 0:1], 0.0))
                    link(V.memset(w_eatt[:, :], 0.0))
                    link(V.memset(ones[:, :], 1.0))
                    link(V.memset(row[:, :], 0.0))
                    link(V.memset(rowscan[:, :], 0.0))
                    for n, (dst_, view) in enumerate(((iota[:, :], i_iota), (pcol[:, :], i_iota[:, 0:1]),
                                                      (tile_no, i_iota[:, 0:TB]), (kfirst, i_iota[:, 0:TB]),
                                                      (slot_no[:, :], block_s[:, :].bitcast(i32)),
                                                      (gidx, block_s[:, :].bitcast(i32)))):
                        dve.wait_ge(s_iota, n + 1)
                        V.tensor_copy(dst_, view).then_inc(s_iota_free, 1)
                        dve.wait_ge(s_iota_free, n + 1)
                    dve.wait_ge(s_id, 1)
                    link(V.tensor_copy(ident_b[:, :], ident[:, :]))
                    dve.wait_ge(s_ints, 32)
                    link(V.tensor_copy(t_dst, i_dst))
                    link(V.tensor_copy(t_src, i_src))
                    dve.wait_ge(s_prev, 16)
                    V.tensor_copy(t_a, i_other).then_inc(s_prev_free, 1)
                    dve.wait_ge(s_prev_free, 1)
                    link(V.tensor_tensor(t_b, t_dst, t_a, ALU.not_equal))
                    link(V.tensor_tensor(t_a, t_b, gidx, ALU.mult))
                    V.tensor_tensor_scan(t_b, reset[:, :], t_a, 0.0, ALU.mult, ALU.max).then_inc(s_rowsrc, 1)
                    link(V.tensor_scalar(i_dst, i_dst, 7, None, ALU.logical_shift_right))
                    dve.wait_ge(s_next, 16)
                    link(V.tensor_copy(t_c, i_dst))
                    link(V.tensor_reduce(bmin, v3(t_c, P), X, ALU.min))
                    link(V.scalar_tensor_tensor(out=t_a, in0=t_c, scalar=float(N_BLOCKS), in1=t_c, op0=ALU.is_lt, op1=ALU.mult))
                    link(V.tensor_reduce(bmax, v3(t_a, P), X, ALU.max))
                    link(V.tensor_tensor(s1, bmax, bmin, ALU.subtract))
                    link(V.tensor_scalar(s2, bmin, float(N_BLOCKS), None, ALU.is_lt))
                    V.scalar_tensor_tensor(out=cnt, in0=s1, scalar=1.0, in1=s2, op0=ALU.add, op1=ALU.mult).then_inc(s_rowsrc, 1)
                    link(V.tensor_copy(t_a, i_other))
                    link(V.tensor_tensor(t_last, t_dst, t_a, ALU.not_equal))

                    def row_in(n):
                        for c in range(4):
                            w = min(512, NS - 512 * c)
                            dve.wait_ge(s_tp, 4 * n + c + 1)
                            V.tensor_copy(row[:, 512 * c:512 * c + w], bank[0][0:1, 0:w]).then_inc(s_rowfree, 1)
                        dve.wait_ge(s_rowfree, 4 * n + 4)

                    row_in(0)
                    V.tensor_tensor_scan(rowscan[:, 1:NS + 1], row[:, 0:NS], row[:, 0:NS], 0.0, ALU.max, ALU.max).then_inc(s_row, 1)
                    dve.wait_ge(s_colps, 1)
                    link(V.tensor_tensor(v3(t_a, P), v3(t_b, P), bank[1][:, 0:TB].unsqueeze(2).broadcast_to((P, TB, P)), ALU.max))
                    link(V.tensor_tensor(t_b, t_a, gidx, ALU.subtract))
                    link(V.scalar_tensor_tensor(out=t_a, in0=t_b, scalar=float(N_EDGES - 1), in1=t_last, op0=ALU.add, op1=ALU.mult))
                    row_in(1)
                    V.tensor_tensor_scan(rowscan[:, 1:NS + 1], reset[0:1, 1:2].broadcast_to((1, NS)), row[:, 0:NS], 0.0,
                                         ALU.mult, ALU.add).then_inc(s_row, 1)
                    dve.wait_ge(s_colps, 2)
                    link(V.tensor_tensor(base, bmin, bank[1][:, 16:16 + TB], ALU.subtract))
                    link(V.tensor_tensor(before, bank[1][:, 16:16 + TB], kfirst, ALU.subtract))
                    link(V.tensor_tensor(end, before, cnt, ALU.add))
                    for k in range(TB):
                        link(V.tensor_scalar(vals[:, 0:2, 0:P], v3(iota[:, :], P), before[:, k:k + 1], None, ALU.is_ge))
                        V.scalar_tensor_tensor(out=sel[:, k, :].rearrange("p (c s) -> p c s", s=P), in0=v3(iota[:, :], P), scalar=end[:, k:k + 1],
                                               in1=vals[:, 0:2, 0:P], op0=ALU.is_lt, op1=ALU.mult).then_inc(s_sel, 1)
                        dve.wait_ge(s_sel, k + 1)
                    for k in range(TB):
                        c = slice(k * P, (k + 1) * P)
                        dve.wait_ge(s_selps, 2 * k + 1)
                        V.tensor_copy(src_s[:, c], bank[2][:, 0:P])
                        V.tensor_copy(last_s[:, c], bank[2][:, 2 * P:3 * P])
                        link(V.tensor_tensor(block_s[:, c], bank[2][:, 3 * P:4 * P], slot_no[:, c], ALU.add))
                        V.scalar_tensor_tensor(out=rel_s[:, c], in0=block_s[:, c], scalar=-float(P), in1=bank[2][:, P:2 * P],
                                               op0=ALU.mult, op1=ALU.add).then_inc(s_selfree, 1)
                        dve.wait_ge(s_selps, 2 * k + 2)
                        V.tensor_copy(i_firstkey[:, c], bank[3][:, 0:P])
                        V.tensor_copy(i_lastkey[0:1, c], bank[3][0:1, P:2 * P])
                        V.tensor_scalar(start_row[:, c], bank[3][0:1, 2 * P:3 * P], float(P), None, ALU.mult).then_inc(s_selfree, 1)
                    dve.wait_ge(s_selfree, 2 * TB)
                    link(V.tensor_scalar(block_1h[:, :], block_s[:, :], pcol[:, 0:1], None, ALU.is_equal))
                    link(V.tensor_scalar(block_row[:, :], block_s[0:1, :], float(N_BLOCKS), None, ALU.min))
                    link(V.scalar_tensor_tensor(out=slot_no[:, :], in0=block_s[:, :], scalar=-float(P), in1=i_firstkey,
                                                op0=ALU.mult, op1=ALU.add))
                    link(V.tensor_scalar(first_ind[:, :], slot_no[:, 0:NS:GS], pcol[:, 0:1], None, ALU.is_equal))
                    link(V.memset(eq_row[:, :], 0.0))
                    link(V.tensor_tensor(eq_row[:, 1:NS], i_firstkey[0:1, 1:NS], i_lastkey[0:1, 0:NS - 1], ALU.is_equal))
                    link(V.tensor_tensor(row[:, 0:NS], i_firstkey[0:1, :], i_lastkey[0:1, :], ALU.is_equal))
                    link(V.tensor_tensor(thru_row[:, :], eq_row[:, :], row[:, 0:NS], ALU.mult))
                    dve.wait_ge(s_wt_ps, 1)
                    link(V.tensor_copy(w_proj[:, 0:NODE_DIM], bank[4][:, 0:NODE_DIM]))
                    link(V.tensor_copy(w_proj[:, NODE_DIM:], bank[4][:, P:P + 2 * HEADS]))
                    link(V.tensor_copy(w_eatt[0:64, 0:HEADS], bank[4][0:64, 2 * P:2 * P + HEADS]))
                    link(V.tensor_copy(w_eatt[64:128, HEADS:2 * HEADS], bank[4][64:128, 2 * P:2 * P + HEADS]))
                    link(V.memset(thru[:, :], 0.0))
                    link(V.memset(lmax[:, :, :], 0.0))
                    link(V.memset(fcont[:, :, :], 0.0))
                    link(V.memset(same[:, :], 0.0))

                @block.tensor
                def _(pe):
                    T = nc.tensor
                    pe.wait_ge(s_id, 1)
                    pe.wait_ge(s_w, 48)
                    pe.wait_ge(s_a, 16 * HEADS)
                    T.transpose(bank[4][:, 0:P], wn[:, :], ident[:, :])
                    T.matmul(bank[4][:, P:P + 2 * HEADS], wn[:, :], a_mat[:, 0:2 * HEADS], start=True, stop=True)
                    T.matmul(bank[4][:, 2 * P:2 * P + HEADS], we2[:, :, :].rearrange("p a d -> p (a d)"),
                             a_mat[:, 2 * HEADS:], start=True, stop=True).then_inc(s_wt_ps, 1)
                    for n, colsof in enumerate((lambda k: v3(t_b, P)[:, k, P - 1:P], lambda k: cnt[:, k:k + 1])):
                        pe.wait_ge(s_rowsrc, n + 1)
                        for c in range(4):
                            if 4 * n + c:
                                pe.wait_ge(s_rowfree, 4 * n + c)
                            for k in range(4 * c, min(4 * c + 4, TB)):
                                last = T.transpose(bank[0][0:1, (k % 4) * P:(k % 4 + 1) * P], colsof(k), ident[:, :])
                            last.then_inc(s_tp, 1)
                        pe.wait_ge(s_row, n + 1)
                        for k in range(TB):
                            last = T.matmul(bank[1][:, 16 * n + k:16 * n + k + 1], rowscan[0:1, k * P:(k + 1) * P], ones[0:1, 0:1],
                                            start=True, stop=True)
                        last.then_inc(s_colps, 1)

                    def bc(t):
                        return t.broadcast_to((P, P))

                    for k in range(TB):
                        parts = [(k - 1, P), (k, 0)] if k else [(0, 0)]
                        pe.wait_ge(s_sel, k + 1)
                        for half, quantities in enumerate((
                                (lambda i: v3(t_src, P)[:, i, :], lambda i: v3(t_dst, P)[:, i, :],
                                 lambda i: v3(t_a, P)[:, i, :], lambda i: bc(base[:, i:i + 1])),
                                (lambda i: bc(v3(t_dst, P)[:, i, 0:1]), lambda i: bc(v3(t_dst, P)[:, i, P - 1:P]),
                                 lambda i: bc(tile_no[:, i:i + 1])))):
                            if k:
                                pe.wait_ge(s_selfree, 2 * (k - 1) + half + 1)
                            for n, q in enumerate(quantities):
                                for i, off in parts:
                                    last = T.matmul(bank[2 + half][:, n * P:(n + 1) * P], q(i), sel[:, i, off:off + P],
                                                    start=(i == parts[0][0]), stop=(i == k))
                            last.then_inc(s_selps, 1)



        with ExitStack() as stage:
            def ssem(name):
                return stage.enter_context(nc.semaphore(name))

            def ssb(name, shape, dt):
                return stage.enter_context(nc.sbuf_tensor(name, shape, dt))

            W = NODE_GROUP
            WP = NODE_DIM + 2 * HEADS
            xg = ssb("xg", [P, 2, W, NODE_DIM], f32)
            xc = ssb("xc", [P, W, NODE_DIM], f32)
            sq = ssb("sq", [P, W, NODE_DIM], f32)
            hn = ssb("hn", [P, W, NODE_DIM], f32)
            hn_t = ssb("hn_t", [P, W * NODE_DIM], f32)
            rows = ssb("rows", [P, 2, W, ROW], f32)
            st = ssb("st", [P, 6, W], f32)
            tres = ssb("tres", [P, 2, N_BLOCKS * HEADS], f32)
            names = ("sum mean centered squared varsum var std rstd hn hn_t_ps hn_t h_ps rows6 rows1 tgt").split()
            s = {n: ssem("node_" + n) for n in names}
            s_x, s_rows = [ssem(f"x_loaded{q}") for q in range(2)], [ssem(f"rows_stored{q}") for q in range(2)]
            s_split, s_ttps, s_acc0 = ssem("tgt_split"), ssem("tgt_transposed"), ssem("acc_zeroed")
            x_g = x.rearrange("(g i p) d -> g p i d", i=W, p=P)
            tab_g = table.rearrange("(g i p) d -> g p i d", i=W, p=P)

            def bcw(t):
                return t.unsqueeze(2).broadcast_to((P, W, NODE_DIM))

            def h_bank(n):
                return bank[2 + n // 3][:, (n % 3) * WP:(n % 3 + 1) * WP]

            with nc.Block() as block:
                @block.sync
                def _(sp):
                    def load(g, q):
                        sp.dma_start(xg[:, q, :, :], x_g[g, :, :, :] if isinstance(g, int) else x_g[ds(g, 1), :, :, :].rearrange("g p i d -> (g p) i d")).then_inc(s_x[q], 16)

                    def store(g, q):
                        sp.dma_start(tab_g[g, :, :, :] if isinstance(g, int) else tab_g[ds(g, 1), :, :, :].rearrange("g p i d -> (g p) i d"), rows[:, q, :, :]).then_inc(s_rows[q], 16)
                    load(0, 0)
                    load(1, 1)
                    for g in range(N_NODE_GROUPS):
                        if g + 2 < N_NODE_GROUPS:
                            sp.wait_ge(s["centered"], g + 1)
                            load(g + 2, g % 2)
                        sp.wait_ge(s["rows1"], g + 1)
                        store(g, g % 2)
                    for q in range(2):
                        sp.wait_ge(s_rows[q], 16 * (N_NODE_GROUPS // 2))

                @block.vector
                def _(dve):
                    V = nc.vector
                    V.memset(acc[:, :], 0.0).then_inc(s_acc0, 1)

                    def evacuate(g, q):
                        dve.wait_ge(s["h_ps"], g + 1)
                        if g >= 2:
                            dve.wait_ge(s_rows[q], 16 * (g // 2))
                        for b in range(2):
                            last = V.tensor_copy(rows[:, q, 3 * b:3 * b + 3, :], v3(bank[2 + b][:, 0:3 * WP], WP)[:, :, 0:ROW])
                        last.then_inc(s["rows6"], 1)
                        V.tensor_copy(rows[:, q, 6, :], h_bank(6)[:, 0:ROW]).then_inc(s["rows1"], 1)
                        for b in range(2):
                            V.tensor_copy(tgt[:, g * W + 3 * b:g * W + 3 * b + 3, :], v3(bank[2 + b][:, 0:3 * WP], WP)[:, :, ROW:WP])
                        V.tensor_copy(tgt[:, g * W + 6, :], h_bank(6)[:, ROW:WP]).then_inc(s["tgt"], 1)

                    for g in range(N_NODE_GROUPS):
                        q = g % 2
                        dve.wait_ge(s_x[q], 16 * (g // 2 + 1))
                        V.reduce_sum(st[:, 0, :], xg[:, q, :, :], X).then_inc(s["sum"], 1)
                        dve.wait_ge(s["sum"], g + 1)
                        V.tensor_scalar(st[:, 1, :], st[:, 0, :], 1.0 / NODE_DIM, None, ALU.mult).then_inc(s["mean"], 1)
                        dve.wait_ge(s["mean"], g + 1)
                        V.tensor_tensor(xc[:, :, :], xg[:, q, :, :], bcw(st[:, 1, :]), ALU.subtract).then_inc(s["centered"], 1)
                        dve.wait_ge(s["squared"], g + 1)
                        V.reduce_sum(st[:, 2, :], sq[:, :, :], X).then_inc(s["varsum"], 1)
                        dve.wait_ge(s["varsum"], g + 1)
                        V.tensor_scalar(st[:, 3, :], st[:, 2, :], 1.0 / NODE_DIM, EPS, ALU.mult, ALU.add).then_inc(s["var"], 1)
                        dve.wait_ge(s["std"], g + 1)
                        V.reciprocal(st[:, 5, :], st[:, 4, :]).then_inc(s["rstd"], 1)
                        dve.wait_ge(s["rstd"], g + 1)
                        if g:
                            dve.wait_ge(s["hn_t_ps"], g)
                        V.tensor_tensor(hn[:, :, :], xc[:, :, :], bcw(st[:, 5, :]), ALU.mult).then_inc(s["hn"], 1)
                        if g:
                            evacuate(g - 1, 1 - q)
                    evacuate(N_NODE_GROUPS - 1, (N_NODE_GROUPS - 1) % 2)
                    dve.wait_ge(s["tgt"], N_NODE_GROUPS)
                    n = 0
                    full = tgt[:, :, :].rearrange("p b h -> p (b h)")
                    for i in range(3):
                        part = tgt_parts[:, i, :, :].rearrange("p b h -> p (b h)")
                        V.tensor_copy(part, full).then_inc(s_split, 1)
                        n += 1
                        dve.wait_ge(s_split, n)
                        if i < 2:
                            V.tensor_tensor(tres[:, i, :], full, part, ALU.subtract).then_inc(s_split, 1)
                            n += 1
                            dve.wait_ge(s_split, n)
                            full = tres[:, i, :]
                    dve.wait_ge(s_ttps, 1)
                    V.tensor_copy(tgt_t[0:N_BLOCKS, :, :], ps_oht[0:N_BLOCKS, 0:3 * HEADS, :]).then_inc(s_split, 1)

                @block.scalar
                def _(act):
                    S = nc.scalar
                    for g in range(N_NODE_GROUPS):
                        act.wait_ge(s["centered"], g + 1)
                        if g:
                            act.wait_ge(s["varsum"], g)
                        S.activation(sq[:, :, :], xc[:, :, :], ACT.Square).then_inc(s["squared"], 1)
                        act.wait_ge(s["var"], g + 1)
                        S.activation(st[:, 4, :], st[:, 3, :], ACT.Sqrt).then_inc(s["std"], 1)
                        act.wait_ge(s["hn_t_ps"], g + 1)
                        if g:
                            act.wait_ge(s["h_ps"], g)
                        S.activation(hn_t[:, 0:4 * P], bank[0][:, :], ACT.Relu)
                        S.activation(hn_t[:, 4 * P:], bank[1][:, 0:3 * P], ACT.Relu).then_inc(s["hn_t"], 1)

                @block.tensor
                def _(pe):
                    T = nc.tensor
                    for g in range(N_NODE_GROUPS):
                        pe.wait_ge(s["hn"], g + 1)
                        if g:
                            pe.wait_ge(s["hn_t"], g)
                        for n in range(W):
                            last = T.transpose(bank[n // 4][:, (n % 4) * P:(n % 4 + 1) * P], hn[:, n, :], ident[:, :])
                        last.then_inc(s["hn_t_ps"], 1)
                        pe.wait_ge(s["hn_t"], g + 1)
                        if g:
                            pe.wait_ge(s["tgt"], g)
                        for n in range(W):
                            last = T.matmul(h_bank(n), hn_t[:, n * P:(n + 1) * P], w_proj[:, :], start=True, stop=True)
                        last.then_inc(s["h_ps"], 1)
                    pe.wait_ge(s_split, 5)
                    for c in range(3 * HEADS):
                        last = T.transpose(ps_oht[0:N_BLOCKS, c, :], tgt_parts[:, c // HEADS, :, c % HEADS], ident_b[:, :])
                    last.then_inc(s_ttps, 1)

        E_BANK = bank[0:2]
        EDGE_BANK, ROW_BANK = bank[2], bank[3]
        SUM_BANK = bank[4:6]
        ps_tgt_slot = E_BANK[0][:, 0:3 * HEADS * GS]
        ps_att_r, ps_rel_r = E_BANK[1][0:HS, 0:P], E_BANK[1][0:HS, P:2 * P]
        ps_se_flat = EDGE_BANK[:, 0:HS]
        ps_se = ps_se_flat.rearrange("p (s h) -> p h s", h=HEADS)
        ps_te = EDGE_BANK[:, 64:64 + HS]
        ps_m = EDGE_BANK[:, 128:128 + HS]
        ps_lrow, ps_frow = ROW_BANK[0:1, 0:HS], ROW_BANK[0:1, 64:64 + HS]
        ps_cols = ROW_BANK[0:HS, 128:130]
        ps_drop = ROW_BANK[:, 132:132 + HEADS]

        with ExitStack() as stage:
            def ssem(name):
                return stage.enter_context(nc.semaphore(name))

            s_ea = [ssem(f"eattr_loaded{q}") for q in range(2)]
            s_g = [ssem(f"rows_gathered{q}") for q in range(2)]
            names = ("idx relg onehot onehot_b oht_ps oht eattr_ps eattr_t0 eattr_t1 tgt_slot_ps tgt_slot se_ps u te_ps z att "
                     "rowsT_ps att_r rel_r same fwd rmax ends_ps thru lmax mfwd fcont mbase mrun cfirst clast drop carry "
                     "cols_ps from_first from_last rm1 mx m_ps arg ex enm alpha_arg alpha scaled lastex vals_h vals sum_ps added pool_go pe_go").split()
            s = {n: ssem(n) for n in names}

            def bsh(t):
                return t.unsqueeze(1).broadcast_to((t.shape[0], HEADS, GS))

            class Group:
                def __init__(self, n, half, par, first=False):
                    self.n, self.half, self.par, self.first = n, half, par, first

            BATCHES = [list(range(t, min(t + 3, GS))) for t in range(0, GS, 3)]
            ENDS = [b[-1] for b in BATCHES]

            with nc.Block() as block:
                @block.sync
                def _(sp):
                    def body(g):
                        for part in range(GS // 8):
                            _, starts = nc.values_load_multi_w_load_instructions(
                                start_row[0:1, ds(g.n * GS + 8 * part, 8)], engines=[mybir.EngineType.SP], min_val=0,
                                max_val=(N_TILES - 1) * P, skip_runtime_bounds_check_because="tile numbers times 128")
                            if part == 0 and not g.first:
                                sp.wait_ge(s["eattr_ps"], g.n - 1)
                            for j in range(8):
                                sp.dma_start(eattr[:, g.par, 8 * part + j, :], ea[ds(starts[j], P), :]).then_inc(s_ea[g.par], 16)
                    body(Group(0, 0, 0, True))
                    body(Group(1, 0, 1, True))
                    with sp.Fori(0, (NG - 2) // 2) as i:
                        body(Group(i * 2 + 2, i + 1, 0))
                        body(Group(i * 2 + 3, i + 1, 1))

                @block.gpsimd
                def _(pool):
                    def body(g):
                        pool.wait_ge(s["idx"], g.n + 1)
                        if not g.first:
                            pool.wait_ge(s["vals"], g.n - 1)
                        pool.sem_inc(s["pool_go"], 1)
                        for j in range(GS):
                            nc.gpsimd.indirect_dma_start(
                                out=gath[:, g.par, j, :], out_offset=None, in_=table,
                                in_offset=bass.IndirectOffsetOnAxis(ap=idx[:, g.par, j:j + 1], axis=0)).then_inc(s_g[g.par], 16)
                    body(Group(0, 0, 0, True))
                    body(Group(1, 0, 1, True))
                    with pool.Fori(0, (NG - 2) // 2) as i:
                        body(Group(i * 2 + 2, i + 1, 0))
                        body(Group(i * 2 + 3, i + 1, 1))

                @block.tensor
                def _(pe):
                    T = nc.tensor

                    def sums(g, lo, hi):
                        for j in range(lo, hi):
                            if j == 0:
                                pe.wait_ge(s["vals"], g.n + 1)
                            if j % 3 == 0 and (j >= 6 or not g.first):
                                back = BATCHES[j // 3 - 2][-1] + 1 - (0 if j >= 6 else GS)
                                pe.wait_ge(s["added"], g.n * GS + back)
                            ins = T.matmul(SUM_BANK[(j // 3) % 2][:, (j % 3) * ACC:(j % 3 + 1) * ACC], onehot[:, g.par, j, :],
                                           vals[:, j, :], start=True, stop=True)
                            if j in ENDS:
                                ins.then_inc(s["sum_ps"], 1)

                    def body(g, prev):
                        def sums_of_last(lo, hi):
                            if prev:
                                sums(prev, lo, hi)

                        pe.wait_ge(s_ea[g.par], (g.half + 1) * (16 * GS))
                        for t in range(2):
                            if not g.first:
                                pe.wait_ge(s["tgt_slot" if t == 0 else "rel_r"], g.n)
                            for j in range(4):
                                last = T.transpose(E_BANK[t][:, j * P:(j + 1) * P],
                                                   eattr[:, g.par, 8 * t + 2 * j:8 * t + 2 * j + 2, :].rearrange("p a d -> p (a d)"), ident[:, :])
                        last.then_inc(s["eattr_ps"], 1)
                        pe.wait_ge(s["eattr_t0"], g.n + 1)
                        for c in range(3 * HEADS):
                            last = T.matmul(ps_tgt_slot[:, c * GS:(c + 1) * GS], tgt_t[0:N_BLOCKS, c, :],
                                            block_1h[0:N_BLOCKS, ds(g.n * GS, GS)], start=True, stop=True)
                        last.then_inc(s["tgt_slot_ps"], 1)
                        sums_of_last(0, 3)
                        if not g.first:
                            pe.wait_ge(s["enm"], g.n)
                        for t in range(2):
                            pe.wait_ge(s[f"eattr_t{t}"], g.n + 1)
                            for j in range(4):
                                c = 4 * t + j
                                last = T.matmul(ps_se_flat[:, 8 * c:8 * c + 8], eattr_t[:, t, j * P:(j + 1) * P], w_eatt[:, :],
                                                start=True, stop=True)
                        last.then_inc(s["se_ps"], 1)
                        pe.wait_ge(s["onehot_b"], g.n + 1)
                        if not g.first:
                            pe.wait_ge(s["oht"], g.n)
                        for j in range(GS):
                            last = T.transpose(ps_oht[:, j, :], onehot_b[:, j, :], ident_b[:, :])
                        last.then_inc(s["oht_ps"], 1)
                        sums_of_last(3, 6)
                        pe.wait_ge(s["oht"], g.n + 1)
                        pe.wait_ge(s["tgt_slot"], g.n + 1)
                        pe.wait_ge(s["u"], g.n + 1)
                        for j in range(GS):
                            for part in range(3):
                                last = T.matmul(ps_te[:, HEADS * j:HEADS * (j + 1)], onehot_t[:, j, :],
                                                tgt_slot[:, HEADS * part:HEADS * (part + 1), j], start=(part == 0), stop=(part == 2))
                        last.then_inc(s["te_ps"], 1)
                        sums_of_last(6, 9)
                        pe.wait_ge(s["att"], g.n + 1)
                        pe.sem_inc(s["pe_go"], 1)
                        T.transpose(ps_att_r, att[:, :, :].rearrange("p h s -> p (h s)"), ident[:, :])
                        T.transpose(ps_rel_r, relg[:, :, :].rearrange("p h s -> p (h s)"), ident[:, :]).then_inc(s["rowsT_ps"], 1)
                        sums_of_last(9, 12)
                        pe.wait_ge(s["rmax"], g.n + 1)
                        if not g.first:
                            pe.wait_ge(s["alpha_arg"], g.n)
                        pe.sem_inc(s["pe_go"], 1)
                        T.transpose(ps_lrow, rmax[:, P - 1:P], ident[0:HS, 0:HS])
                        T.transpose(ps_frow, rmax[:, 0:1], ident[0:HS, 0:HS]).then_inc(s["ends_ps"], 1)
                        sums_of_last(12, 15)
                        pe.wait_ge(s["clast"], g.n + 1)
                        pe.wait_ge(s["drop"], g.n + 1)
                        T.matmul(ps_cols[:, 0:1], cfirst[0:1, :, :].rearrange("p h s -> p (h s)"), ones[0:1, 0:1], start=True, stop=True)
                        T.matmul(ps_cols[:, 1:2], clast[0:1, :, :].rearrange("p h s -> p (h s)"), ones[0:1, 0:1], start=True, stop=True)
                        T.matmul(ps_drop, ones[0:1, :], drop[0:1, :], start=True, stop=True).then_inc(s["cols_ps"], 1)
                        sums_of_last(15, GS)
                        pe.wait_ge(s["mx"], g.n + 1)
                        pe.sem_inc(s["pe_go"], 1)
                        T.transpose(ps_m, mx[:, :], ident[0:HS, 0:HS]).then_inc(s["m_ps"], 1)

                    body(Group(0, 0, 0, True), None)
                    body(Group(1, 0, 1), Group(0, 0, 0, True))
                    with pe.Fori(0, (NG - 2) // 2) as i:
                        one, two = Group(i * 2 + 2, i + 1, 0), Group(i * 2 + 3, i + 1, 1)
                        body(one, Group(i * 2 + 1, i, 1))
                        body(two, one)
                    final = Group(NG - 1, NG // 2 - 1, 1)
                    sums(final, 0, GS)

                @block.scalar
                def _(act):
                    S = nc.scalar
                    S.copy(idx[:, 0, :], src_s[:, 0:GS]).then_inc(s["idx"], 1)
                    S.copy(idx[:, 1, :], src_s[:, GS:2 * GS]).then_inc(s["idx"], 1)

                    def body(g, more=True):
                        act.wait_ge(s["eattr_ps"], g.n + 1)
                        if not g.first:
                            act.wait_ge(s["se_ps"], g.n)
                        for t in range(2):
                            S.copy(eattr_t[:, t, :], E_BANK[t][:, :]).then_inc(s[f"eattr_t{t}"], 1)
                        act.wait_ge(s["tgt_slot_ps"], g.n + 1)
                        if not g.first:
                            act.wait_ge(s["te_ps"], g.n)
                        S.copy(tgt_slot[:, :, :].rearrange("p c s -> p (c s)"), ps_tgt_slot).then_inc(s["tgt_slot"], 1)
                        act.wait_ge(s["onehot"], g.n + 1)
                        if not g.first:
                            act.wait_ge(s["oht_ps"], g.n)
                        S.copy(onehot_b[:, :, :], onehot[:, g.par, :, :]).then_inc(s["onehot_b"], 1)
                        act.wait_ge(s["oht_ps"], g.n + 1)
                        S.copy(onehot_t[:, :, :], ps_oht[:, :, :]).then_inc(s["oht"], 1)
                        act.wait_ge(s["rowsT_ps"], g.n + 1)
                        S.activation(att_r[:, :], ps_att_r, ACT.Relu).then_inc(s["att_r"], 1)
                        S.copy(rel_r[:, :], ps_rel_r).then_inc(s["rel_r"], 1)
                        if more:
                            act.wait_ge(s_g[g.par], (g.half + 1) * (16 * GS))
                            S.copy(idx[:, g.par, :], src_s[:, ds((g.n + 2) * GS, GS)]).then_inc(s["idx"], 1)
                        act.wait_ge(s["arg"], g.n + 1)
                        S.activation(ex[:, :, :], arg[:, :, :], ACT.Exp).then_inc(s["ex"], 1)
                        S.activation(enm[:, :, :].rearrange("p h s -> p (h s)"), ps_m, ACT.Exp, scale=-1.0).then_inc(s["enm"], 1)
                        act.wait_ge(s["alpha_arg"], g.n + 1)
                        S.activation(alpha[:, :], alpha_arg[:, :], ACT.Exp).then_inc(s["alpha"], 1)

                    body(Group(0, 0, 0, True))
                    body(Group(1, 0, 1))
                    with act.Fori(0, (NG - 4) // 2) as i:
                        body(Group(i * 2 + 2, i + 1, 0))
                        body(Group(i * 2 + 3, i + 1, 1))
                    body(Group(NG - 2, NG // 2 - 1, 0), more=False)
                    body(Group(NG - 1, NG // 2 - 1, 1), more=False)

                @block.vector
                def _(dve):
                    V = nc.vector

                    def accumulate(g, blocks, lo, hi):
                        for j in range(lo, hi):
                            a_blk = acc_b[:, ds(blocks[j], 1), :].rearrange("p b c -> p (b c)")
                            if j == 0:
                                dve.wait_ge(s["alpha"], g.n + 1)
                                if not g.first:
                                    dve.wait_ge(s["added"], g.n * GS)
                                a_h = a_blk.rearrange("p (h c) -> p h c", h=HEADS)
                                V.tensor_tensor(a_h, a_h, alpha[:, :].unsqueeze(2).broadcast_to((P, HEADS, HC)), ALU.mult).then_inc(s["scaled"], 1)
                                dve.wait_ge(s["scaled"], g.n + 1)
                            else:
                                dve.wait_ge(s["added"], g.n * GS + j)
                            if j % 3 == 0:
                                dve.wait_ge(s["sum_ps"], g.n * len(BATCHES) + (j // 3 + 1))
                            V.tensor_tensor(a_blk, a_blk, SUM_BANK[(j // 3) % 2][:, (j % 3) * ACC:(j % 3 + 1) * ACC], ALU.add).then_inc(s["added"], 1)

                    def load_blocks(g):
                        blocks = []
                        for part in range(GS // 8):
                            _, b = nc.values_load_multi_w_load_instructions(
                                block_row[0:1, ds(g.n * GS + 8 * part, 8)], engines=[mybir.EngineType.DVE], min_val=0,
                                max_val=N_BLOCKS, skip_runtime_bounds_check_because="clamped to N_BLOCKS in stage 1")
                            blocks += b
                        return blocks

                    def body(g, prev):
                        blocks = load_blocks(prev) if prev else None

                        def add(lo, hi):
                            if prev:
                                accumulate(prev, blocks, lo, hi)

                        slots = ds(g.n * GS, GS)
                        thru_v = thru[0:1, 0:HEADS * (GS + 1)].rearrange("p (h s) -> p h s", h=HEADS)
                        if not g.first:
                            dve.wait_ge(s["rowsT_ps"], g.n)
                        V.tensor_copy(relg[:, :, :], bsh(rel_s[:, slots])).then_inc(s["relg"], 1)
                        dve.wait_ge(s["relg"], g.n + 1)
                        V.tensor_tensor(onehot[:, g.par, :, :], iota[:, 0:P].unsqueeze(1).broadcast_to((P, GS, P)),
                                        relg[:, 0, :].unsqueeze(2).broadcast_to((P, GS, P)), ALU.is_equal).then_inc(s["onehot"], 1)
                        V.tensor_copy(thru_v[:, :, 1:GS + 1], bsh(thru_row[0:1, slots])).then_inc(s["thru"], 1)
                        add(0, 3)
                        dve.wait_ge(s["se_ps"], g.n + 1)
                        dve.wait_ge(s_g[g.par], (g.half + 1) * (16 * GS))
                        V.tensor_tensor(u[:, :, :], gath[:, g.par, :, NODE_DIM:ROW].rearrange("p s h -> p h s"), ps_se, ALU.add).then_inc(s["u"], 1)
                        add(3, 6)
                        dve.wait_ge(s["u"], g.n + 1)
                        dve.wait_ge(s["te_ps"], g.n + 1)
                        V.tensor_tensor(z[:, :, :], u[:, :, :], ps_te.rearrange("p (s h) -> p h s", h=HEADS), ALU.add).then_inc(s["z"], 1)
                        dve.wait_ge(s["z"], g.n + 1)
                        V.scalar_tensor_tensor(out=att[:, :, :].rearrange("p h s -> p (h s)"), in0=z[:, :, :].rearrange("p h s -> p (h s)"), scalar=0.2,
                                               in1=z[:, :, :].rearrange("p h s -> p (h s)"), op0=ALU.mult, op1=ALU.max).then_inc(s["att"], 1)
                        add(6, 9)
                        dve.wait_ge(s["rel_r"], g.n + 1)
                        V.tensor_tensor(same[:, 1:P], rel_r[:, 1:P], rel_r[:, 0:P - 1], ALU.is_equal).then_inc(s["same"], 1)
                        dve.wait_ge(s["same"], g.n + 1)
                        V.tensor_tensor_scan(fmax[:, :], same[:, 0:P], att_r[:, :], 0.0, ALU.mult, ALU.max).then_inc(s["fwd"], 1)
                        dve.wait_ge(s["fwd"], g.n + 1)
                        V.tensor_tensor_scan(rmax[:, ::-1], same[:, P:0:-1], fmax[:, ::-1], 0.0, ALU.mult, ALU.max).then_inc(s["rmax"], 1)
                        add(9, 12)
                        dve.wait_ge(s["ends_ps"], g.n + 1)
                        if not g.first:
                            dve.wait_ge(s["carry"], g.n)
                        V.tensor_copy(lmax[:, :, 1:GS + 1], ps_lrow.rearrange("p (h s) -> p h s", h=HEADS)).then_inc(s["lmax"], 1)
                        V.tensor_tensor(fcont[:, :, 0:GS], ps_frow.rearrange("p (h s) -> p h s", h=HEADS), bsh(eq_row[0:1, slots]), ALU.mult).then_inc(s["fcont"], 1)
                        dve.wait_ge(s["lmax"], g.n + 1)
                        dve.wait_ge(s["thru"], g.n + 1)
                        V.tensor_tensor_scan(mfwd[:, :], thru[0:1, 0:HEADS * (GS + 1)], lmax[:, :, :].rearrange("p h s -> p (h s)"), 0.0,
                                             ALU.mult, ALU.max).then_inc(s["mfwd"], 1)
                        dve.wait_ge(s["mfwd"], g.n + 1)
                        dve.wait_ge(s["fcont"], g.n + 1)
                        V.tensor_tensor(mbase[:, :], mfwd[:, :], fcont[:, :, :].rearrange("p h s -> p (h s)"), ALU.max).then_inc(s["mbase"], 1)
                        dve.wait_ge(s["mbase"], g.n + 1)
                        n1 = HEADS * (GS + 1)
                        V.tensor_tensor_scan(mrun[:, :, :].rearrange("p h s -> p (h s)")[:, ::-1], thru[0:1, n1:0:-1], mbase[:, ::-1], 0.0,
                                             ALU.mult, ALU.max).then_inc(s["mrun"], 1)
                        dve.wait_ge(s["mrun"], g.n + 1)
                        V.tensor_tensor(cfirst[:, :, :], mrun[:, :, 0:GS], bsh(eq_row[0:1, slots]), ALU.mult).then_inc(s["cfirst"], 1)
                        V.tensor_copy(clast[:, :, :], mrun[:, :, 1:GS + 1]).then_inc(s["clast"], 1)
                        V.tensor_tensor(drop[:, :], lmax[:, :, 0], mrun[:, :, 0], ALU.subtract).then_inc(s["drop"], 1)
                        dve.wait_ge(s["drop"], g.n + 1)
                        V.tensor_copy(lmax[:, :, 0:1], mrun[:, :, GS:GS + 1]).then_inc(s["carry"], 1)
                        add(12, 15)
                        dve.wait_ge(s["cols_ps"], g.n + 1)
                        V.tensor_scalar(from_first[:, :], rel_r[:, :], rel_r[:, 0:1], ps_cols[:, 0:1], ALU.is_equal, ALU.mult).then_inc(s["from_first"], 1)
                        V.tensor_scalar(from_last[:, :], rel_r[:, :], rel_r[:, P - 1:P], ps_cols[:, 1:2], ALU.is_equal, ALU.mult).then_inc(s["from_last"], 1)
                        dve.wait_ge(s["from_first"], g.n + 1)
                        V.tensor_tensor(rm1[:, :], rmax[:, :], from_first[:, :], ALU.max).then_inc(s["rm1"], 1)
                        dve.wait_ge(s["from_last"], g.n + 1)
                        dve.wait_ge(s["rm1"], g.n + 1)
                        V.tensor_tensor(mx[:, :], rm1[:, :], from_last[:, :], ALU.max).then_inc(s["mx"], 1)
                        add(15, GS)
                        dve.wait_ge(s["m_ps"], g.n + 1)
                        V.tensor_tensor(arg[:, :, :].rearrange("p h s -> p (h s)"), att[:, :, :].rearrange("p h s -> p (h s)"), ps_m,
                                        ALU.subtract).then_inc(s["arg"], 1)
                        if prev:
                            dve.wait_ge(s["scaled"], g.n)
                        V.tensor_scalar(alpha_arg[:, :], ps_drop, first_ind[:, ds(g.n, 1)], None, ALU.mult).then_inc(s["alpha_arg"], 1)
                        dve.wait_ge(s["ex"], g.n + 1)
                        vh = vals[:, :, :].rearrange("p s (h c) -> p s h c", h=HEADS)
                        V.tensor_tensor(vh[:, :, :, 0:HD], gath[:, g.par, :, 0:NODE_DIM].rearrange("p s (h c) -> p s h c", h=HEADS),
                                        ex[:, :, :].rearrange("p h s -> p s h").unsqueeze(3).broadcast_to((P, GS, HEADS, HD)), ALU.mult).then_inc(s["vals_h"], 1)
                        dve.wait_ge(s["enm"], g.n + 1)
                        V.tensor_tensor(lastex[:, :, :], enm[:, :, :], bsh(last_s[:, slots]), ALU.mult).then_inc(s["lastex"], 1)
                        dve.wait_ge(s["lastex"], g.n + 1)
                        dve.wait_ge(s["vals_h"], g.n + 1)
                        V.tensor_tensor(vh[:, :, :, HD], ex[:, :, :].rearrange("p h s -> p s h"), lastex[:, :, :].rearrange("p h s -> p s h"),
                                        ALU.add).then_inc(s["vals"], 1)

                    body(Group(0, 0, 0, True), None)
                    body(Group(1, 0, 1), Group(0, 0, 0, True))
                    with dve.Fori(0, (NG - 2) // 2) as i:
                        one, two = Group(i * 2 + 2, i + 1, 0), Group(i * 2 + 3, i + 1, 1)
                        body(one, Group(i * 2 + 1, i, 1))
                        body(two, one)
                    final = Group(NG - 1, NG // 2 - 1, 1)
                    accumulate(final, load_blocks(final), 0, GS)

        with ExitStack() as stage:
            def ssem(name):
                return stage.enter_context(nc.semaphore(name))

            def ssb(name, shape, dt):
                return stage.enter_context(nc.sbuf_tensor(name, shape, dt))

            W = 2 * NODE_GROUP
            n_out = N_BLOCKS // W
            xo = ssb("xo", [P, 2, W, NODE_DIM], f32)
            yo = ssb("yo", [P, 2, W, NODE_DIM], f32)
            den = ssb("den", [P, 2, W * HEADS], f32)
            s_x, s_out = [ssem(f"x_again{q}") for q in range(2)], [ssem(f"stored{q}") for q in range(2)]
            s_e, s_d, s_r, s_m, s_y = ssem("empty_nodes"), ssem("denominators"), ssem("reciprocals"), ssem("normalised"), ssem("results")
            x_g = x.rearrange("(g i p) d -> g p i d", i=W, p=P)
            out_g = out.rearrange("(g i p) d -> g p i d", i=W, p=P)
            with nc.Block() as block:
                @block.sync
                def _(sp):
                    for g in range(n_out):
                        if g >= 2:
                            sp.wait_ge(s_y, g - 1)
                        sp.dma_start(xo[:, g % 2, :, :], x_g[g, :, :, :]).then_inc(s_x[g % 2], 16)

                @block.scalar
                def _(act):
                    for g in range(n_out):
                        act.wait_ge(s_y, g + 1)
                        act.dma_start(out_g[g, :, :, :], yo[:, g % 2, :, :]).then_inc(s_out[g % 2], 16)
                    for q in range(2):
                        act.wait_ge(s_out[q], 16 * len(range(q, n_out, 2)))

                @block.vector
                def _(dve):
                    V = nc.vector
                    for g in range(n_out):
                        q = g % 2
                        a4 = acc_b[:, g * W:(g + 1) * W, :].rearrange("p b (h c) -> p (b h) c", h=HEADS)
                        V.tensor_scalar(den[:, 0, :], a4[:, :, HD], 0.0, None, ALU.is_equal).then_inc(s_e, 1)
                        dve.wait_ge(s_e, g + 1)
                        V.tensor_tensor(den[:, 1, :], a4[:, :, HD], den[:, 0, :], ALU.add).then_inc(s_d, 1)
                        dve.wait_ge(s_d, g + 1)
                        V.reciprocal(den[:, 0, :], den[:, 1, :]).then_inc(s_r, 1)
                        dve.wait_ge(s_r, g + 1)
                        if g >= 2:
                            dve.wait_ge(s_out[q], 16 * (g // 2))
                        y3 = yo[:, q, :, :].rearrange("p b (h c) -> p (b h) c", h=HEADS)
                        V.tensor_tensor(y3, a4[:, :, 0:HD], den[:, 0, :].unsqueeze(2).broadcast_to((P, W * HEADS, HD)), ALU.mult).then_inc(s_m, 1)
                        dve.wait_ge(s_m, g + 1)
                        dve.wait_ge(s_x[q], 16 * (g // 2 + 1))
                        V.tensor_tensor(yo[:, q, :, :], yo[:, q, :, :], xo[:, q, :, :], ALU.add).then_inc(s_y, 1)


def kernel(**inputs):
    import numpy as np
    import concourse.bacc as bacc
    from concourse.bass_utils import run_bass_kernel_spmd

    x = np.zeros((N_BLOCKS * P, NODE_DIM), np.float32)
    x[:N_NODES] = inputs["x"]
    src = np.zeros((NS * P,), np.int32)
    src[:N_EDGES] = inputs["src"]
    dst = np.full((NS * P + 2,), PAD_DST, np.int32)
    dst[1:N_EDGES + 1] = inputs["dst"]
    ea = np.zeros((N_TILES * P, EDGE_DIM), np.float32)
    ea[:N_EDGES] = inputs["edge_attr_64"]
    arrays = {"x_in": x, "src_in": src, "dst_in": dst, "edge_attr_in": ea,
              "w_node_in": np.ascontiguousarray(inputs["L0_gnn_W_node"]),
              "w_edge_in": np.ascontiguousarray(inputs["L0_gnn_W_edge"]),
              "a_in": np.ascontiguousarray(inputs["L0_gnn_a"])}
    nc = bacc.Bacc("TRN2", target_bir_lowering=False, num_devices=1)
    args = [nc.dram_tensor(n, v.shape, mybir.dt.from_np(v.dtype), kind="ExternalInput").ap() for n, v in arrays.items()]
    out = nc.dram_tensor("out_dram", (N_BLOCKS * P, NODE_DIM), mybir.dt.float32, kind="ExternalOutput").ap()
    gat_kernel(nc, *args, out)
    r = run_bass_kernel_spmd(nc, [arrays], core_ids=[0])
    return r.results[0]["out_dram"][:N_NODES]
```

```python
import concourse.bass as bass
from concourse import mybir
from contextlib import ExitStack

N_NODES, N_EDGES, NODE_DIM, EDGE_DIM = 12500, 200000, 128, 64
HEADS, HD = 4, 32
P = 128
N_BLOCKS = -(-N_NODES // P)
N_TILES = -(-N_EDGES // P)
TB = -(-(N_TILES + N_BLOCKS - 1) // P)
NS = TB * P
GS = 16
NG = NS // GS
RING = 3
HS = HEADS * GS
ROW = NODE_DIM + HEADS
HC = HD + 1
ACC = HEADS * HC
PAD_DST = 1 << 20
NODE_GROUP = 7
N_NODE_GROUPS = N_BLOCKS // NODE_GROUP
EPS = 1e-5


def gat_kernel(nc, x, src, dst, ea, w_node, w_edge, a, out):
    f32, bf16, i32 = mybir.dt.float32, mybir.dt.bfloat16, mybir.dt.int32
    ALU = mybir.AluOpType
    ACT = mybir.ActivationFunctionType
    X = mybir.AxisListType.X
    ds = bass.ds

    table = nc.dram_tensor("node_table", [N_BLOCKS * P, ROW], f32, kind="Internal").ap()

    ctx = ExitStack()
    with ctx:
        def sb(name, shape, dt):
            return ctx.enter_context(nc.sbuf_tensor(name, shape, dt))

        def pb(name, shape, dt=f32):
            return ctx.enter_context(nc.psum_tensor(name, shape, dt))

        def sem(name):
            return ctx.enter_context(nc.semaphore(name))

        acc = sb("acc", [P, (N_BLOCKS + 1) * ACC], f32)
        acc_b = acc[:, :].rearrange("p (b c) -> p b c", c=ACC)
        gath = sb("gath", [P, RING, GS, ROW], f32)
        vals = sb("vals", [P, GS, ACC], f32)
        onehot = sb("onehot", [P, RING, GS, P], f32)
        onehot_b = sb("onehot_b", [P, GS, P], bf16)
        onehot_t = sb("onehot_t", [P, GS, P], bf16)
        eattr = sb("eattr", [P, RING, GS, EDGE_DIM], f32)
        eattr_t = sb("eattr_t", [P, 2, 4 * P], f32)
        idx = sb("idx", [P, RING, GS], i32)
        src_s = sb("src_s", [P, NS], f32)
        rel_s = sb("rel_s", [P, NS], f32)
        last_s = sb("last_s", [P, NS], f32)
        block_1h = sb("block_1h", [P, NS], bf16)
        first_ind = sb("first_ind", [P, NG], f32)
        eq_row = sb("eq_row", [1, NS], bf16)
        thru_row = sb("thru_row", [1, NS], bf16)
        block_row = sb("block_row", [1, NS], i32)
        start_row = sb("start_row", [1, NS], i32)
        ident = sb("ident", [P, P], f32)
        ident_b = sb("ident_b", [P, P], bf16)
        iota = sb("iota", [P, 2 * P], f32)
        pcol = sb("pcol", [P, 1], f32)
        ones = sb("ones", [1, P], f32)
        w_proj = sb("w_proj", [P, NODE_DIM + 2 * HEADS], f32)
        w_eatt = sb("w_eatt", [P, 2 * HEADS], f32)
        a_mat = sb("a_mat", [P, 3 * HEADS], f32)
        wn = sb("wn", [P, NODE_DIM], f32)
        we2 = sb("we2", [P, 2, EDGE_DIM], f32)
        tgt = sb("tgt", [P, N_BLOCKS, HEADS], f32)
        tgt_parts = sb("tgt_parts", [P, 3, N_BLOCKS, HEADS], bf16)
        tgt_t = sb("tgt_t", [P, 3 * HEADS, P], bf16)
        tgt_slot = sb("tgt_slot", [P, 3 * HEADS, GS], bf16)
        relg = sb("relg", [P, HEADS, GS], f32)
        u = sb("u", [P, HEADS, GS], f32)
        z = sb("z", [P, HEADS, GS], f32)
        att = sb("att", [P, RING, HEADS, GS], f32)
        arg = sb("arg", [P, HEADS, GS], f32)
        ex = sb("ex", [P, HEADS, GS], f32)
        enm = sb("enm", [P, HEADS, GS], f32)
        lastex = sb("lastex", [P, HEADS, GS], f32)
        att_r = sb("att_r", [HS, RING, P], f32)
        rel_r = sb("rel_r", [HS, RING, P], f32)
        same = sb("same", [HS, P + 1], f32)
        fmax = sb("fmax", [HS, P], f32)
        rmax = sb("rmax", [HS, P], f32)
        from_first = sb("from_first", [HS, P], f32)
        from_last = sb("from_last", [HS, P], f32)
        rm1 = sb("rm1", [HS, P], f32)
        mx = sb("mx", [HS, P], f32)
        thru = sb("thru", [1, HEADS * (GS + 1) + 1], f32)
        lmax = sb("lmax", [1, HEADS, GS + 1], f32)
        mfwd = sb("mfwd", [1, HEADS * (GS + 1)], f32)
        fcont = sb("fcont", [1, HEADS, GS + 1], f32)
        mbase = sb("mbase", [1, HEADS * (GS + 1)], f32)
        mrun = sb("mrun", [1, HEADS, GS + 1], f32)
        cfirst = sb("cfirst", [1, HEADS, GS], f32)
        clast = sb("clast", [1, HEADS, GS], f32)
        drop = sb("drop", [1, HEADS], f32)
        alpha_arg = sb("alpha_arg", [P, HEADS], f32)
        alpha = sb("alpha", [P, HEADS], f32)

        bank = [pb(f"bank{i}", [P, 512]) for i in range(6)]
        ps_oht = pb("ps_oht", [P, GS, P], bf16)

        def v3(t, cols):
            return t.rearrange("p (a c) -> p a c", c=cols)

        def tmp(n):
            off = [0]
            for m in (NS,) * 5 + (2 * P * TB,):
                off.append(off[-1] + m)
            return acc[:, off[n]:off[n + 1]]

        t_dst, t_a, t_b, t_c, t_last = tmp(0), tmp(1), tmp(2), tmp(3), tmp(4)
        sel = tmp(5).rearrange("p (k s) -> p k s", k=TB)
        oh_flat, gath_flat, ea_flat = (t[:, :, :, :].rearrange("p a s r -> p (a s r)") for t in (onehot, gath, eattr))
        t_src = gath_flat[:, 0:NS]
        gidx = gath_flat[:, NS:2 * NS]
        i_dst = oh_flat[:, 0:NS].bitcast(i32)
        i_other = oh_flat[:, NS:2 * NS].bitcast(i32)
        i_src = vals[:, :, :].rearrange("p s c -> p (s c)")[:, 0:NS].bitcast(i32)
        t_hi = onehot_b[:, :, :].rearrange("p s c -> p (s c)").bitcast(f32)
        i_iota = eattr_t[:, 0, 0:2 * P].bitcast(i32)
        reset = src_s
        i_firstkey, i_lastkey = oh_flat[:, 0:NS], oh_flat[:, NS:2 * NS]

        with ExitStack() as stage:
            def ssem(name):
                return stage.enter_context(nc.semaphore(name))

            def ssb(name, shape, dt):
                return stage.enter_context(nc.sbuf_tensor(name, shape, dt))

            small = ssb("small", [P, 16, TB], f32)
            bmin, bmax, cnt, before, end, base, tile_no, kfirst = (small[:, i, :] for i in range(8))
            s1, s2 = small[:, 8, :], small[:, 9, :]
            row = ssb("row", [1, NS + 1], f32)
            rowscan = ea_flat[0:1, 0:NS + 1]
            slot_no = oh_flat[:, 2 * NS:3 * NS]
            block_s = gath_flat[:, 2 * NS:3 * NS]

            s_w, s_ints, s_amat0, s_a = ssem("weights_loaded"), ssem("ints_loaded"), ssem("a_zeroed"), ssem("a_loaded")
            s_prev, s_next, s_prev_free = ssem("prev_loaded"), ssem("next_loaded"), ssem("other_ints_free")
            s_id, s_id0, s_iota, s_iota_free = ssem("ident_made"), ssem("ident_zeroed"), ssem("iota_made"), ssem("iota_free")
            s_dve, s_act = ssem("dve_step"), ssem("act_step")
            s_wt_ps, s_tp, s_colps, s_selps = ssem("weights_projected"), ssem("rows_transposed"), ssem("columns_back"), ssem("slots_selected")
            s_rowsrc, s_row, s_rowfree, s_sel, s_selfree = ssem("row_source"), ssem("row_scanned"), ssem("row_bank_free"), ssem("sel_made"), ssem("sel_bank_free")

            def tiles(n):
                return dst[n:n + NS * P].rearrange("(k q p) -> q k p", q=P, p=P)

            with nc.Block() as block:
                @block.sync
                def _(sp):
                    sp.dma_start(v3(i_dst, P), tiles(1)).then_inc(s_ints, 16)
                    sp.dma_start(v3(i_src, P), src.rearrange("(k q p) -> q k p", q=P, p=P)).then_inc(s_ints, 16)
                    sp.dma_start(v3(i_other, P), tiles(0)).then_inc(s_prev, 16)
                    sp.dma_start(wn[:, :], w_node).then_inc(s_w, 16)
                    for j in range(2):
                        sp.dma_start(we2[:, j, :], w_edge).then_inc(s_w, 16)
                    sp.wait_ge(s_amat0, 1)
                    for h in range(HEADS):
                        sp.dma_start(a_mat[h * HD:(h + 1) * HD, h:3 * HEADS:HEADS],
                                     a[h, :].rearrange("(s d) -> d s", s=3),
                                     allow_slow_non_contiguous=True).then_inc(s_a, 16)
                    sp.wait_ge(s_prev_free, 1)
                    sp.dma_start(v3(i_other, P), tiles(2)).then_inc(s_next, 16)

                @block.gpsimd
                def _(pool):
                    pool.memset(ident[:, :], 0.0).then_inc(s_id0, 1)
                    pool.wait_ge(s_id0, 1)
                    pool.affine_select(out=ident[:, :], in_=ident[:, :], compare_op=ALU.not_equal, fill=1.0,
                                       base=0, pattern=[[-1, P]], channel_multiplier=1).then_inc(s_id, 1)
                    for n, (view, pattern, base_, mult) in enumerate((
                            (i_iota, [[1, 2 * P]], 0, 0), (i_iota[:, 0:1], [[1, 1]], 0, 1),
                            (i_iota[:, 0:TB], [[P, TB]], 0, 1), (i_iota[:, 0:TB], [[P, TB]], 0, 0))):
                        if n:
                            pool.wait_ge(s_iota_free, n)
                        pool.iota(view, pattern=pattern, base=base_, channel_multiplier=mult).then_inc(s_iota, 1)
                    pool.wait_ge(s_iota_free, 4)
                    pool.iota(block_s[:, :].bitcast(i32), pattern=[[1, NS]], base=0, channel_multiplier=0).then_inc(s_iota, 1)
                    pool.wait_ge(s_iota_free, 5)
                    pool.iota(v3(block_s[:, :].bitcast(i32), P), pattern=[[P * P, TB], [1, P]], base=0,
                              channel_multiplier=P).then_inc(s_iota, 1)

                @block.vector
                def _(dve):
                    step = [0]

                    def link(ins):
                        step[0] += 1
                        ins.then_inc(s_dve, 1)
                        dve.wait_ge(s_dve, step[0])

                    V = nc.vector
                    V.memset(a_mat[:, :], 0.0).then_inc(s_amat0, 1)
                    link(V.memset(reset[:, :], 1.0))
                    link(V.memset(v3(reset[:, :], P)[:, :, 0:1], 0.0))
                    link(V.memset(w_eatt[:, :], 0.0))
                    link(V.memset(ones[:, :], 1.0))
                    link(V.memset(row[:, :], 0.0))
                    link(V.memset(rowscan[:, :], 0.0))
                    for n, (dst_, view) in enumerate(((iota[:, :], i_iota), (pcol[:, :], i_iota[:, 0:1]),
                                                      (tile_no, i_iota[:, 0:TB]), (kfirst, i_iota[:, 0:TB]),
                                                      (slot_no[:, :], block_s[:, :].bitcast(i32)),
                                                      (gidx, block_s[:, :].bitcast(i32)))):
                        dve.wait_ge(s_iota, n + 1)
                        V.tensor_copy(dst_, view).then_inc(s_iota_free, 1)
                        dve.wait_ge(s_iota_free, n + 1)
                    dve.wait_ge(s_id, 1)
                    link(V.tensor_copy(ident_b[:, :], ident[:, :]))
                    dve.wait_ge(s_ints, 32)
                    link(V.tensor_copy(t_dst, i_dst))
                    link(V.tensor_copy(t_src, i_src))
                    dve.wait_ge(s_prev, 16)
                    V.tensor_copy(t_a, i_other).then_inc(s_prev_free, 1)
                    dve.wait_ge(s_prev_free, 1)
                    link(V.tensor_tensor(t_b, t_dst, t_a, ALU.not_equal))
                    link(V.tensor_tensor(t_a, t_b, gidx, ALU.mult))
                    V.tensor_tensor_scan(t_b, reset[:, :], t_a, 0.0, ALU.mult, ALU.max).then_inc(s_rowsrc, 1)
                    link(V.tensor_scalar(i_dst, i_dst, 7, None, ALU.logical_shift_right))
                    dve.wait_ge(s_next, 16)
                    link(V.tensor_copy(t_c, i_dst))
                    link(V.tensor_reduce(bmin, v3(t_c, P), X, ALU.min))
                    link(V.scalar_tensor_tensor(out=t_a, in0=t_c, scalar=float(N_BLOCKS), in1=t_c, op0=ALU.is_lt, op1=ALU.mult))
                    link(V.tensor_reduce(bmax, v3(t_a, P), X, ALU.max))
                    link(V.tensor_tensor(s1, bmax, bmin, ALU.subtract))
                    link(V.tensor_scalar(s2, bmin, float(N_BLOCKS), None, ALU.is_lt))
                    V.scalar_tensor_tensor(out=cnt, in0=s1, scalar=1.0, in1=s2, op0=ALU.add, op1=ALU.mult).then_inc(s_rowsrc, 1)
                    link(V.tensor_copy(t_a, i_other))
                    link(V.tensor_tensor(t_last, t_dst, t_a, ALU.not_equal))

                    def row_in(n):
                        for c in range(4):
                            w = min(512, NS - 512 * c)
                            dve.wait_ge(s_tp, 4 * n + c + 1)
                            V.tensor_copy(row[:, 512 * c:512 * c + w], bank[0][0:1, 0:w]).then_inc(s_rowfree, 1)
                        dve.wait_ge(s_rowfree, 4 * n + 4)

                    row_in(0)
                    V.tensor_tensor_scan(rowscan[:, 1:NS + 1], row[:, 0:NS], row[:, 0:NS], 0.0, ALU.max, ALU.max).then_inc(s_row, 1)
                    dve.wait_ge(s_colps, 1)
                    link(V.tensor_tensor(v3(t_a, P), v3(t_b, P), bank[1][:, 0:TB].unsqueeze(2).broadcast_to((P, TB, P)), ALU.max))
                    link(V.tensor_tensor(t_b, t_a, gidx, ALU.subtract))
                    link(V.scalar_tensor_tensor(out=t_a, in0=t_b, scalar=float(N_EDGES - 1), in1=t_last, op0=ALU.add, op1=ALU.mult))
                    row_in(1)
                    V.tensor_tensor_scan(rowscan[:, 1:NS + 1], reset[0:1, 1:2].broadcast_to((1, NS)), row[:, 0:NS], 0.0,
                                         ALU.mult, ALU.add).then_inc(s_row, 1)
                    dve.wait_ge(s_colps, 2)
                    link(V.tensor_tensor(base, bmin, bank[1][:, 16:16 + TB], ALU.subtract))
                    link(V.tensor_tensor(before, bank[1][:, 16:16 + TB], kfirst, ALU.subtract))
                    link(V.tensor_tensor(end, before, cnt, ALU.add))
                    for k in range(TB):
                        link(V.tensor_scalar(vals[:, 0:2, 0:P], v3(iota[:, :], P), before[:, k:k + 1], None, ALU.is_ge))
                        V.scalar_tensor_tensor(out=sel[:, k, :].rearrange("p (c s) -> p c s", s=P), in0=v3(iota[:, :], P), scalar=end[:, k:k + 1],
                                               in1=vals[:, 0:2, 0:P], op0=ALU.is_lt, op1=ALU.mult).then_inc(s_sel, 1)
                        dve.wait_ge(s_sel, k + 1)
                    for k in range(TB):
                        c = slice(k * P, (k + 1) * P)
                        dve.wait_ge(s_selps, 2 * k + 1)
                        V.tensor_copy(src_s[:, c], bank[2][:, 0:P])
                        V.tensor_copy(last_s[:, c], bank[2][:, 2 * P:3 * P])
                        link(V.tensor_tensor(block_s[:, c], bank[2][:, 3 * P:4 * P], slot_no[:, c], ALU.add))
                        V.scalar_tensor_tensor(out=rel_s[:, c], in0=block_s[:, c], scalar=-float(P), in1=bank[2][:, P:2 * P],
                                               op0=ALU.mult, op1=ALU.add).then_inc(s_selfree, 1)
                        dve.wait_ge(s_selps, 2 * k + 2)
                        V.tensor_copy(i_firstkey[:, c], bank[3][:, 0:P])
                        V.tensor_copy(i_lastkey[0:1, c], bank[3][0:1, P:2 * P])
                        V.tensor_scalar(start_row[:, c], bank[3][0:1, 2 * P:3 * P], float(P), None, ALU.mult).then_inc(s_selfree, 1)
                    dve.wait_ge(s_selfree, 2 * TB)
                    link(V.tensor_scalar(block_1h[:, :], block_s[:, :], pcol[:, 0:1], None, ALU.is_equal))
                    link(V.tensor_scalar(block_row[:, :], block_s[0:1, :], float(N_BLOCKS), None, ALU.min))
                    link(V.scalar_tensor_tensor(out=slot_no[:, :], in0=block_s[:, :], scalar=-float(P), in1=i_firstkey,
                                                op0=ALU.mult, op1=ALU.add))
                    link(V.tensor_scalar(first_ind[:, :], slot_no[:, 0:NS:GS], pcol[:, 0:1], None, ALU.is_equal))
                    link(V.memset(eq_row[:, :], 0.0))
                    link(V.tensor_tensor(eq_row[:, 1:NS], i_firstkey[0:1, 1:NS], i_lastkey[0:1, 0:NS - 1], ALU.is_equal))
                    link(V.tensor_tensor(row[:, 0:NS], i_firstkey[0:1, :], i_lastkey[0:1, :], ALU.is_equal))
                    link(V.tensor_tensor(thru_row[:, :], eq_row[:, :], row[:, 0:NS], ALU.mult))
                    dve.wait_ge(s_wt_ps, 1)
                    link(V.tensor_copy(w_proj[:, 0:NODE_DIM], bank[4][:, 0:NODE_DIM]))
                    link(V.tensor_copy(w_proj[:, NODE_DIM:], bank[4][:, P:P + 2 * HEADS]))
                    link(V.tensor_copy(w_eatt[0:64, 0:HEADS], bank[4][0:64, 2 * P:2 * P + HEADS]))
                    link(V.tensor_copy(w_eatt[64:128, HEADS:2 * HEADS], bank[4][64:128, 2 * P:2 * P + HEADS]))
                    link(V.memset(thru[:, :], 0.0))
                    link(V.memset(lmax[:, :, :], 0.0))
                    link(V.memset(fcont[:, :, :], 0.0))
                    link(V.memset(same[:, :], 0.0))

                @block.tensor
                def _(pe):
                    T = nc.tensor
                    pe.wait_ge(s_id, 1)
                    pe.wait_ge(s_w, 48)
                    pe.wait_ge(s_a, 16 * HEADS)
                    T.transpose(bank[4][:, 0:P], wn[:, :], ident[:, :])
                    T.matmul(bank[4][:, P:P + 2 * HEADS], wn[:, :], a_mat[:, 0:2 * HEADS], start=True, stop=True)
                    T.matmul(bank[4][:, 2 * P:2 * P + HEADS], we2[:, :, :].rearrange("p a d -> p (a d)"),
                             a_mat[:, 2 * HEADS:], start=True, stop=True).then_inc(s_wt_ps, 1)
                    for n, colsof in enumerate((lambda k: v3(t_b, P)[:, k, P - 1:P], lambda k: cnt[:, k:k + 1])):
                        pe.wait_ge(s_rowsrc, n + 1)
                        for c in range(4):
                            if 4 * n + c:
                                pe.wait_ge(s_rowfree, 4 * n + c)
                            for k in range(4 * c, min(4 * c + 4, TB)):
                                last = T.transpose(bank[0][0:1, (k % 4) * P:(k % 4 + 1) * P], colsof(k), ident[:, :])
                            last.then_inc(s_tp, 1)
                        pe.wait_ge(s_row, n + 1)
                        for k in range(TB):
                            last = T.matmul(bank[1][:, 16 * n + k:16 * n + k + 1], rowscan[0:1, k * P:(k + 1) * P], ones[0:1, 0:1],
                                            start=True, stop=True)
                        last.then_inc(s_colps, 1)

                    def bc(t):
                        return t.broadcast_to((P, P))

                    for k in range(TB):
                        parts = [(k - 1, P), (k, 0)] if k else [(0, 0)]
                        pe.wait_ge(s_sel, k + 1)
                        for half, quantities in enumerate((
                                (lambda i: v3(t_src, P)[:, i, :], lambda i: v3(t_dst, P)[:, i, :],
                                 lambda i: v3(t_a, P)[:, i, :], lambda i: bc(base[:, i:i + 1])),
                                (lambda i: bc(v3(t_dst, P)[:, i, 0:1]), lambda i: bc(v3(t_dst, P)[:, i, P - 1:P]),
                                 lambda i: bc(tile_no[:, i:i + 1])))):
                            if k:
                                pe.wait_ge(s_selfree, 2 * (k - 1) + half + 1)
                            for n, q in enumerate(quantities):
                                for i, off in parts:
                                    last = T.matmul(bank[2 + half][:, n * P:(n + 1) * P], q(i), sel[:, i, off:off + P],
                                                    start=(i == parts[0][0]), stop=(i == k))
                            last.then_inc(s_selps, 1)



        with ExitStack() as stage:
            def ssem(name):
                return stage.enter_context(nc.semaphore(name))

            def ssb(name, shape, dt):
                return stage.enter_context(nc.sbuf_tensor(name, shape, dt))

            W = NODE_GROUP
            WP = NODE_DIM + 2 * HEADS
            WD = W * NODE_DIM
            xg = gath_flat[:, 0:2 * WD].rearrange("p (q w d) -> p q w d", q=2, w=W)
            sq, hn = (gath_flat[:, n * WD:(n + 1) * WD].rearrange("p (w d) -> p w d", w=W) for n in (3, 4))
            xc = [gath_flat[:, n * WD:(n + 1) * WD].rearrange("p (w d) -> p w d", w=W) for n in (2, 6)]
            hn_t = gath_flat[:, 5 * WD:6 * WD]
            rows = oh_flat[:, 0:2 * W * ROW].rearrange("p (q w r) -> p q w r", q=2, w=W)
            tres = oh_flat[:, 2 * W * ROW:2 * W * ROW + 2 * N_BLOCKS * HEADS].rearrange("p (a b) -> p a b", a=2)
            st = ssb("st", [P, 6, W], f32)
            names = ("sum mean centered squared varsum var std rstd hn hn_t_ps hn_t h_ps rows6 rows1 tgt").split()
            s = {n: ssem("node_" + n) for n in names}
            s_x, s_rows = [ssem(f"x_loaded{q}") for q in range(2)], [ssem(f"rows_stored{q}") for q in range(2)]
            s_split, s_ttps, s_acc0 = ssem("tgt_split"), ssem("tgt_transposed"), ssem("acc_zeroed")
            x_g = x.rearrange("(g i p) d -> g p i d", i=W, p=P)
            tab_g = table.rearrange("(g i p) d -> g p i d", i=W, p=P)

            def bcw(t):
                return t.unsqueeze(2).broadcast_to((P, W, NODE_DIM))

            def h_bank(n):
                return bank[2 + n // 3][:, (n % 3) * WP:(n % 3 + 1) * WP]

            with nc.Block() as block:
                @block.gpsimd
                def _(pool):
                    pool.memset(acc[:, :], 0.0).then_inc(s_acc0, 1)

                @block.sync
                def _(sp):
                    def load(g, q):
                        sp.dma_start(xg[:, q, :, :], x_g[g, :, :, :] if isinstance(g, int) else x_g[ds(g, 1), :, :, :].rearrange("g p i d -> (g p) i d")).then_inc(s_x[q], 16)

                    def store(g, q):
                        sp.dma_start(tab_g[g, :, :, :] if isinstance(g, int) else tab_g[ds(g, 1), :, :, :].rearrange("g p i d -> (g p) i d"), rows[:, q, :, :]).then_inc(s_rows[q], 16)
                    load(0, 0)
                    load(1, 1)
                    for g in range(N_NODE_GROUPS):
                        if g + 2 < N_NODE_GROUPS:
                            sp.wait_ge(s["centered"], g + 1)
                            load(g + 2, g % 2)
                        if g:
                            sp.wait_ge(s["rows1"], g)
                            store(g - 1, (g - 1) % 2)
                    sp.wait_ge(s["rows1"], N_NODE_GROUPS)
                    store(N_NODE_GROUPS - 1, (N_NODE_GROUPS - 1) % 2)
                    for q in range(2):
                        sp.wait_ge(s_rows[q], 16 * (N_NODE_GROUPS // 2))

                @block.vector
                def _(dve):
                    V = nc.vector
                    def evacuate(g, q):
                        dve.wait_ge(s["h_ps"], g + 1)
                        if g >= 2:
                            dve.wait_ge(s_rows[q], 16 * (g // 2))
                        for b in range(2):
                            last = V.tensor_copy(rows[:, q, 3 * b:3 * b + 3, :], v3(bank[2 + b][:, 0:3 * WP], WP)[:, :, 0:ROW])
                        last.then_inc(s["rows6"], 1)
                        V.tensor_copy(rows[:, q, 6, :], h_bank(6)[:, 0:ROW]).then_inc(s["rows1"], 1)
                        for b in range(2):
                            V.tensor_copy(tgt[:, g * W + 3 * b:g * W + 3 * b + 3, :], v3(bank[2 + b][:, 0:3 * WP], WP)[:, :, ROW:WP])
                        V.tensor_copy(tgt[:, g * W + 6, :], h_bank(6)[:, ROW:WP]).then_inc(s["tgt"], 1)

                    def center(g):
                        q = g % 2
                        dve.wait_ge(s_x[q], 16 * (g // 2 + 1))
                        V.reduce_sum(st[:, 0, :], xg[:, q, :, :], X).then_inc(s["sum"], 1)
                        dve.wait_ge(s["sum"], g + 1)
                        V.tensor_scalar(st[:, 1, :], st[:, 0, :], 1.0 / NODE_DIM, None, ALU.mult).then_inc(s["mean"], 1)
                        dve.wait_ge(s["mean"], g + 1)
                        if g >= 2:
                            dve.wait_ge(s["hn"], g - 1)
                        V.tensor_tensor(xc[q], xg[:, q, :, :], bcw(st[:, 1, :]), ALU.subtract).then_inc(s["centered"], 1)

                    center(0)
                    for g in range(N_NODE_GROUPS):
                        q = g % 2
                        dve.wait_ge(s["squared"], g + 1)
                        V.reduce_sum(st[:, 2, :], sq[:, :, :], X).then_inc(s["varsum"], 1)
                        dve.wait_ge(s["varsum"], g + 1)
                        V.tensor_scalar(st[:, 3, :], st[:, 2, :], 1.0 / NODE_DIM, EPS, ALU.mult, ALU.add).then_inc(s["var"], 1)
                        if g + 1 < N_NODE_GROUPS:
                            center(g + 1)
                        dve.wait_ge(s["std"], g + 1)
                        V.reciprocal(st[:, 5, :], st[:, 4, :]).then_inc(s["rstd"], 1)
                        dve.wait_ge(s["rstd"], g + 1)
                        if g:
                            dve.wait_ge(s["hn_t_ps"], g)
                        V.tensor_tensor(hn[:, :, :], xc[q], bcw(st[:, 5, :]), ALU.mult).then_inc(s["hn"], 1)
                        if g:
                            evacuate(g - 1, 1 - q)
                    evacuate(N_NODE_GROUPS - 1, (N_NODE_GROUPS - 1) % 2)
                    dve.wait_ge(s["tgt"], N_NODE_GROUPS)
                    n = 0
                    full = tgt[:, :, :].rearrange("p b h -> p (b h)")
                    for i in range(3):
                        part = tgt_parts[:, i, :, :].rearrange("p b h -> p (b h)")
                        V.tensor_copy(part, full).then_inc(s_split, 1)
                        n += 1
                        dve.wait_ge(s_split, n)
                        if i < 2:
                            V.tensor_tensor(tres[:, i, :], full, part, ALU.subtract).then_inc(s_split, 1)
                            n += 1
                            dve.wait_ge(s_split, n)
                            full = tres[:, i, :]
                    dve.wait_ge(s_ttps, 1)
                    V.tensor_copy(tgt_t[0:N_BLOCKS, :, :], ps_oht[0:N_BLOCKS, 0:3 * HEADS, :]).then_inc(s_split, 1)

                @block.scalar
                def _(act):
                    S = nc.scalar
                    def square(g):
                        act.wait_ge(s["centered"], g + 1)
                        if g:
                            act.wait_ge(s["varsum"], g)
                        S.activation(sq[:, :, :], xc[g % 2], ACT.Square).then_inc(s["squared"], 1)

                    square(0)
                    for g in range(N_NODE_GROUPS):
                        act.wait_ge(s["var"], g + 1)
                        S.activation(st[:, 4, :], st[:, 3, :], ACT.Sqrt).then_inc(s["std"], 1)
                        if g + 1 < N_NODE_GROUPS:
                            square(g + 1)
                        act.wait_ge(s["hn_t_ps"], g + 1)
                        if g:
                            act.wait_ge(s["h_ps"], g)
                        S.activation(hn_t[:, 0:4 * P], bank[0][:, :], ACT.Relu)
                        S.activation(hn_t[:, 4 * P:], bank[1][:, 0:3 * P], ACT.Relu).then_inc(s["hn_t"], 1)

                @block.tensor
                def _(pe):
                    T = nc.tensor
                    for g in range(N_NODE_GROUPS):
                        pe.wait_ge(s["hn"], g + 1)
                        if g:
                            pe.wait_ge(s["hn_t"], g)
                        for n in range(W):
                            last = T.transpose(bank[n // 4][:, (n % 4) * P:(n % 4 + 1) * P], hn[:, n, :], ident[:, :])
                        last.then_inc(s["hn_t_ps"], 1)
                        pe.wait_ge(s["hn_t"], g + 1)
                        if g:
                            pe.wait_ge(s["tgt"], g)
                        for n in range(W):
                            last = T.matmul(h_bank(n), hn_t[:, n * P:(n + 1) * P], w_proj[:, :], start=True, stop=True)
                        last.then_inc(s["h_ps"], 1)
                    pe.wait_ge(s_split, 5)
                    for c in range(3 * HEADS):
                        last = T.transpose(ps_oht[0:N_BLOCKS, c, :], tgt_parts[:, c // HEADS, :, c % HEADS], ident_b[:, :])
                    last.then_inc(s_ttps, 1)

        E_BANK = bank[0:2]
        EDGE_BANK, ROW_BANK = bank[2], bank[3]
        SUM_BANK = bank[4:6]
        ps_tgt_slot = E_BANK[0][:, 0:3 * HEADS * GS]
        ps_att_r, ps_rel_r = E_BANK[1][0:HS, 0:P], E_BANK[1][0:HS, P:2 * P]
        ps_se_flat = EDGE_BANK[:, 0:HS]
        ps_se = ps_se_flat.rearrange("p (s h) -> p h s", h=HEADS)
        ps_te = E_BANK[0][:, 256:256 + HS]
        ps_lrow, ps_frow = ROW_BANK[0:1, 0:HS], ROW_BANK[0:1, 64:64 + HS]
        ps_cols = ROW_BANK[0:HS, 128:130]
        ps_drop = ROW_BANK[:, 132:132 + HEADS]
        ps_m = ROW_BANK[:, 192:192 + HS]

        with ExitStack() as stage:
            def ssem(name):
                return stage.enter_context(nc.semaphore(name))

            s_ea = [ssem(f"eattr_loaded{q}") for q in range(RING)]
            s_g = [ssem(f"rows_gathered{q}") for q in range(RING)]
            names = ("idx relg onehot onehot_b oht_ps oht eattr_ps eattr_t0 eattr_t1 tgt_slot_ps tgt_slot se_ps u te_ps z att "
                     "rowsT_ps att_r rel_r same fwd rmax ends_ps thru lmax mfwd fcont mbase mrun cfirst clast drop carry "
                     "cols_ps from_first from_last rm1 mx m_ps arg ex enm alpha_arg alpha scaled lastex vals_h vals sum_ps added "
                     "pool_go pe_go").split()
            s = {n: ssem(n) for n in names}

            def bsh(t):
                return t.unsqueeze(1).broadcast_to((t.shape[0], HEADS, GS))

            def flat(t):
                return t.rearrange("p h s -> p (h s)")

            class Group:
                def __init__(self, k, i=None):
                    self.n = k if i is None else i * RING + k
                    self.uses = k // RING if i is None else i + k // RING
                    self.slot = k % RING
                    self.first = i is None and k == 0

            BATCHES = [list(range(t, min(t + 3, GS))) for t in range(0, GS, 3)]
            ENDS = [b[-1] for b in BATCHES]
            FRONT = RING + 2
            assert (NG - FRONT) % RING == 0

            with nc.Block() as block:
                @block.sync
                def _(sp):
                    def body(g, wait=True):
                        for part in range(GS // 8):
                            _, starts = nc.values_load_multi_w_load_instructions(
                                start_row[0:1, ds(g.n * GS + 8 * part, 8)], engines=[mybir.EngineType.SP], min_val=0,
                                max_val=(N_TILES - 1) * P, skip_runtime_bounds_check_because="tile numbers times 128")
                            if part == 0 and wait:
                                sp.wait_ge(s["eattr_ps"], g.n - (RING - 1))
                            for j in range(8):
                                sp.dma_start(eattr[:, g.slot, 8 * part + j, :], ea[ds(starts[j], P), :]).then_inc(s_ea[g.slot], 16)
                    for k in range(FRONT):
                        body(Group(k), wait=k >= RING)
                    with sp.Fori(0, (NG - FRONT) // RING) as i:
                        for k in range(RING):
                            body(Group(FRONT + k, i))

                @block.gpsimd
                def _(pool):
                    def body(g, wait=True):
                        pool.wait_ge(s["idx"], g.n + 1)
                        if wait:
                            pool.wait_ge(s["vals"], g.n - (RING - 1))
                        pool.sem_inc(s["pool_go"], 1)
                        for j in range(GS):
                            nc.gpsimd.indirect_dma_start(
                                out=gath[:, g.slot, j, :], out_offset=None, in_=table,
                                in_offset=bass.IndirectOffsetOnAxis(ap=idx[:, g.slot, j:j + 1], axis=0)).then_inc(s_g[g.slot], 16)
                    for k in range(FRONT):
                        body(Group(k), wait=k >= RING)
                    with pool.Fori(0, (NG - FRONT) // RING) as i:
                        for k in range(RING):
                            body(Group(FRONT + k, i))

                def iterations(eng, start, body, finish):
                    start(Group(0), Group(1))
                    body(Group(0), None, Group(1), Group(2))
                    body(Group(1), Group(0), Group(2), Group(3))
                    with eng.Fori(0, (NG - FRONT) // RING) as i:
                        for k in range(2, 2 + RING):
                            body(Group(k, i), Group(k - 1, i), Group(k + 1, i), Group(k + 2, i))
                    for k in range(NG - RING, NG):
                        body(Group(k), Group(k - 1), *(Group(k + n) if k + n < NG else None for n in (1, 2)))
                    finish(Group(NG - 1))

                @block.tensor
                def _(pe):
                    T = nc.tensor

                    def edge_transposes(g):
                        pe.wait_ge(s_ea[g.slot], (g.uses + 1) * (16 * GS))
                        for t in range(2):
                            if not g.first:
                                pe.wait_ge(s["z" if t == 0 else "rel_r"], g.n)
                            for j in range(4):
                                last = T.transpose(E_BANK[t][:, j * P:(j + 1) * P],
                                                   eattr[:, g.slot, 8 * t + 2 * j:8 * t + 2 * j + 2, :].rearrange("p a d -> p (a d)"), ident[:, :])
                        last.then_inc(s["eattr_ps"], 1)

                    def slot_targets(g):
                        pe.wait_ge(s["eattr_t0"], g.n + 1)
                        for c in range(3 * HEADS):
                            last = T.matmul(ps_tgt_slot[:, c * GS:(c + 1) * GS], tgt_t[0:N_BLOCKS, c, :],
                                            block_1h[0:N_BLOCKS, ds(g.n * GS, GS)], start=True, stop=True)
                        last.then_inc(s["tgt_slot_ps"], 1)

                    def edge_parts(g, t):
                        if t == 0 and not g.first:
                            pe.wait_ge(s["u"], g.n)
                        pe.wait_ge(s[f"eattr_t{t}"], g.n + 1)
                        for j in range(4):
                            c = 4 * t + j
                            last = T.matmul(ps_se_flat[:, 8 * c:8 * c + 8], eattr_t[:, t, j * P:(j + 1) * P], w_eatt[:, :],
                                            start=True, stop=True)
                        if t == 1:
                            last.then_inc(s["se_ps"], 1)

                    def onehot_transposes(g):
                        pe.wait_ge(s["onehot_b"], g.n + 1)
                        if not g.first:
                            pe.wait_ge(s["oht"], g.n)
                        for j in range(GS):
                            last = T.transpose(ps_oht[:, j, :], onehot_b[:, j, :], ident_b[:, :])
                        last.then_inc(s["oht_ps"], 1)

                    def target_parts(g):
                        pe.wait_ge(s["oht"], g.n + 1)
                        pe.wait_ge(s["tgt_slot"], g.n + 1)
                        for j in range(GS):
                            for part in range(3):
                                last = T.matmul(ps_te[:, HEADS * j:HEADS * (j + 1)], onehot_t[:, j, :],
                                                tgt_slot[:, HEADS * part:HEADS * (part + 1), j], start=(part == 0), stop=(part == 2))
                        last.then_inc(s["te_ps"], 1)

                    def to_rows(g):
                        pe.wait_ge(s["att"], g.n + 1)
                        pe.wait_ge(s["relg"], g.n + 1)
                        pe.sem_inc(s["pe_go"], 1)
                        T.transpose(ps_att_r, flat(att[:, g.slot, :, :]), ident[:, :])
                        T.transpose(ps_rel_r, flat(relg[:, :, :]), ident[:, :]).then_inc(s["rowsT_ps"], 1)

                    def ends(g):
                        pe.wait_ge(s["rmax"], g.n + 1)
                        if not g.first:
                            pe.wait_ge(s["enm"], g.n)
                        pe.sem_inc(s["pe_go"], 1)
                        T.transpose(ps_lrow, rmax[:, P - 1:P], ident[0:HS, 0:HS])
                        T.transpose(ps_frow, rmax[:, 0:1], ident[0:HS, 0:HS]).then_inc(s["ends_ps"], 1)

                    def to_columns(g):
                        pe.wait_ge(s["drop"], g.n + 1)
                        T.matmul(ps_cols[:, 0:1], flat(cfirst[0:1, :, :]), ones[0:1, 0:1], start=True, stop=True)
                        T.matmul(ps_cols[:, 1:2], flat(clast[0:1, :, :]), ones[0:1, 0:1], start=True, stop=True)
                        T.matmul(ps_drop, ones[0:1, :], drop[0:1, :], start=True, stop=True).then_inc(s["cols_ps"], 1)

                    def maxima(g):
                        pe.wait_ge(s["mx"], g.n + 1)
                        pe.wait_ge(s["alpha_arg"], g.n + 1)
                        pe.sem_inc(s["pe_go"], 1)
                        T.transpose(ps_m, mx[:, :], ident[0:HS, 0:HS]).then_inc(s["m_ps"], 1)

                    def sums(g, batch):
                        if g is None:
                            return
                        if batch == 0:
                            pe.wait_ge(s["vals"], g.n + 1)
                        if batch >= 2:
                            pe.wait_ge(s["added"], g.n * GS + (ENDS[batch - 2] + 1))
                        elif not g.first:
                            pe.wait_ge(s["added"], g.n * GS + (ENDS[batch - 2] + 1 - GS))
                        for j in BATCHES[batch]:
                            last = T.matmul(SUM_BANK[batch % 2][:, (j % 3) * ACC:(j % 3 + 1) * ACC], onehot[:, g.slot, j, :],
                                            vals[:, j, :], start=True, stop=True)
                        last.then_inc(s["sum_ps"], 1)

                    def body(g, prev, nxt, second):
                        def ahead(step, *more):
                            if nxt:
                                step(nxt, *more)
                        sums(prev, 0)
                        ends(g)
                        sums(prev, 1)
                        sums(prev, 2)
                        to_columns(g)
                        ahead(onehot_transposes)
                        maxima(g)
                        sums(prev, 3)
                        sums(prev, 4)
                        ahead(target_parts)
                        sums(prev, 5)
                        ahead(to_rows)
                        if second:
                            edge_transposes(second)
                            slot_targets(second)
                            edge_parts(second, 0)
                            edge_parts(second, 1)

                    def start(g, second):
                        edge_transposes(g)
                        slot_targets(g)
                        onehot_transposes(g)
                        edge_parts(g, 0)
                        edge_parts(g, 1)
                        target_parts(g)
                        to_rows(g)
                        edge_transposes(second)
                        slot_targets(second)
                        edge_parts(second, 0)
                        edge_parts(second, 1)

                    iterations(pe, start, body, lambda g: [sums(g, b) for b in range(len(BATCHES))])

                @block.scalar
                def _(act):
                    S = nc.scalar
                    for k in range(RING):
                        S.copy(idx[:, k, :], src_s[:, k * GS:(k + 1) * GS]).then_inc(s["idx"], 1)

                    def edges_out(g):
                        act.wait_ge(s["eattr_ps"], g.n + 1)
                        if not g.first:
                            act.wait_ge(s["se_ps"], g.n)
                        for t in range(2):
                            S.copy(eattr_t[:, t, :], E_BANK[t][:, :]).then_inc(s[f"eattr_t{t}"], 1)
                        act.wait_ge(s["tgt_slot_ps"], g.n + 1)
                        if not g.first:
                            act.wait_ge(s["te_ps"], g.n)
                        S.copy(flat(tgt_slot[:, :, :]), ps_tgt_slot).then_inc(s["tgt_slot"], 1)

                    def onehot_cast(g):
                        act.wait_ge(s["onehot"], g.n + 1)
                        if not g.first:
                            act.wait_ge(s["oht_ps"], g.n)
                        S.copy(onehot_b[:, :, :], onehot[:, g.slot, :, :]).then_inc(s["onehot_b"], 1)

                    def onehot_out(g):
                        act.wait_ge(s["oht_ps"], g.n + 1)
                        S.copy(onehot_t[:, :, :], ps_oht[:, :, :]).then_inc(s["oht"], 1)

                    def group_keys(g):
                        if not g.first:
                            act.wait_ge(s["rowsT_ps"], g.n)
                        S.copy(relg[:, :, :], bsh(rel_s[:, ds(g.n * GS, GS)])).then_inc(s["relg"], 1)

                    def rows_out(g):
                        act.wait_ge(s["rowsT_ps"], g.n + 1)
                        S.activation(att_r[:, g.slot, :], ps_att_r, ACT.Relu).then_inc(s["att_r"], 1)
                        S.copy(rel_r[:, g.slot, :], ps_rel_r).then_inc(s["rel_r"], 1)

                    def exponentials(g):
                        act.wait_ge(s["arg"], g.n + 1)
                        S.activation(ex[:, :, :], arg[:, :, :], ACT.Exp).then_inc(s["ex"], 1)
                        S.activation(flat(enm[:, :, :]), ps_m, ACT.Exp, scale=-1.0).then_inc(s["enm"], 1)
                        if not g.first:
                            act.wait_ge(s["scaled"], g.n)
                        S.activation(alpha[:, :], alpha_arg[:, :], ACT.Exp).then_inc(s["alpha"], 1)

                    def next_idx(g):
                        act.wait_ge(s_g[g.slot], (g.uses + 1) * (16 * GS))
                        S.copy(idx[:, g.slot, :], src_s[:, ds((g.n + RING) * GS, GS)]).then_inc(s["idx"], 1)

                    def body(g, prev, nxt, second):
                        if nxt:
                            onehot_out(nxt)
                            group_keys(nxt)
                        exponentials(g)
                        if nxt:
                            rows_out(nxt)
                        if second:
                            edges_out(second)
                        if not (isinstance(g.n, int) and g.n + RING >= NG):
                            next_idx(g)
                        if second:
                            onehot_cast(second)

                    def start(g, second):
                        for step in (edges_out, onehot_cast, onehot_out, group_keys, rows_out):
                            step(g)
                        edges_out(second)
                        onehot_cast(second)

                    iterations(act, start, body, lambda g: None)

                @block.vector
                def _(dve):
                    V = nc.vector
                    n1 = HEADS * (GS + 1)
                    thru_v = thru[0:1, 0:n1].rearrange("p (h s) -> p h s", h=HEADS)

                    def slots(g):
                        return ds(g.n * GS, GS)

                    def load_blocks(g):
                        blocks = []
                        for part in range(GS // 8):
                            _, b = nc.values_load_multi_w_load_instructions(
                                block_row[0:1, ds(g.n * GS + 8 * part, 8)], engines=[mybir.EngineType.DVE], min_val=0,
                                max_val=N_BLOCKS, skip_runtime_bounds_check_because="clamped to N_BLOCKS in stage 1")
                            blocks += b
                        return blocks

                    def block_acc(b):
                        return acc_b[:, ds(b, 1), :].rearrange("p b c -> p (b c)")

                    def rescale(g, blocks):
                        dve.wait_ge(s["alpha"], g.n + 1)
                        if not g.first:
                            dve.wait_ge(s["added"], g.n * GS)
                        a_h = block_acc(blocks[0]).rearrange("p (h c) -> p h c", h=HEADS)
                        V.tensor_tensor(a_h, a_h, alpha[:, :].unsqueeze(2).broadcast_to((P, HEADS, HC)), ALU.mult).then_inc(s["scaled"], 1)

                    def add(g, blocks, j):
                        if j == 0:
                            dve.wait_ge(s["scaled"], g.n + 1)
                        else:
                            dve.wait_ge(s["added"], g.n * GS + j)
                        if j % 3 == 0:
                            dve.wait_ge(s["sum_ps"], g.n * len(BATCHES) + (j // 3 + 1))
                        a_blk = block_acc(blocks[j])
                        V.tensor_tensor(a_blk, a_blk, SUM_BANK[(j // 3) % 2][:, (j % 3) * ACC:(j % 3 + 1) * ACC], ALU.add).then_inc(s["added"], 1)

                    def make_onehot(g):
                        V.tensor_tensor(onehot[:, g.slot, :, :], iota[:, 0:P].unsqueeze(1).broadcast_to((P, GS, P)),
                                        rel_s[:, slots(g)].unsqueeze(2).broadcast_to((P, GS, P)), ALU.is_equal).then_inc(s["onehot"], 1)

                    def add_source(g):
                        dve.wait_ge(s["se_ps"], g.n + 1)
                        dve.wait_ge(s_g[g.slot], (g.uses + 1) * (16 * GS))
                        V.tensor_tensor(u[:, :, :], gath[:, g.slot, :, NODE_DIM:ROW].rearrange("p s h -> p h s"), ps_se, ALU.add).then_inc(s["u"], 1)

                    def add_target(g):
                        dve.wait_ge(s["u"], g.n + 1)
                        dve.wait_ge(s["te_ps"], g.n + 1)
                        V.tensor_tensor(z[:, :, :], u[:, :, :], ps_te.rearrange("p (s h) -> p h s", h=HEADS), ALU.add).then_inc(s["z"], 1)

                    def leaky(g):
                        dve.wait_ge(s["z"], g.n + 1)
                        V.scalar_tensor_tensor(out=flat(att[:, g.slot, :, :]), in0=flat(z[:, :, :]), scalar=0.2,
                                               in1=flat(z[:, :, :]), op0=ALU.mult, op1=ALU.max).then_inc(s["att"], 1)

                    def same_key(g):
                        dve.wait_ge(s["rel_r"], g.n + 1)
                        r = rel_r[:, g.slot, :]
                        V.tensor_tensor(same[:, 1:P], r[:, 1:P], r[:, 0:P - 1], ALU.is_equal).then_inc(s["same"], 1)

                    def run_max_forward(g):
                        dve.wait_ge(s["same"], g.n + 1)
                        V.tensor_tensor_scan(fmax[:, :], same[:, 0:P], att_r[:, g.slot, :], 0.0, ALU.mult, ALU.max).then_inc(s["fwd"], 1)

                    def run_max(g):
                        dve.wait_ge(s["fwd"], g.n + 1)
                        V.tensor_tensor_scan(rmax[:, ::-1], same[:, P:0:-1], fmax[:, ::-1], 0.0, ALU.mult, ALU.max).then_inc(s["rmax"], 1)

                    def thru_flags(g):
                        V.tensor_copy(thru_v[:, :, 1:GS + 1], bsh(thru_row[0:1, slots(g)])).then_inc(s["thru"], 1)

                    def end_values(g):
                        dve.wait_ge(s["ends_ps"], g.n + 1)
                        if not g.first:
                            dve.wait_ge(s["carry"], g.n)
                        V.tensor_copy(lmax[:, :, 1:GS + 1], ps_lrow.rearrange("p (h s) -> p h s", h=HEADS)).then_inc(s["lmax"], 1)
                        V.tensor_tensor(fcont[:, :, 0:GS], ps_frow.rearrange("p (h s) -> p h s", h=HEADS), bsh(eq_row[0:1, slots(g)]),
                                        ALU.mult).then_inc(s["fcont"], 1)

                    def ends_forward(g):
                        dve.wait_ge(s["lmax"], g.n + 1)
                        dve.wait_ge(s["thru"], g.n + 1)
                        V.tensor_tensor_scan(mfwd[:, :], thru[0:1, 0:n1], flat(lmax[:, :, :]), 0.0, ALU.mult, ALU.max).then_inc(s["mfwd"], 1)

                    def ends_base(g):
                        dve.wait_ge(s["mfwd"], g.n + 1)
                        dve.wait_ge(s["fcont"], g.n + 1)
                        V.tensor_tensor(mbase[:, :], mfwd[:, :], flat(fcont[:, :, :]), ALU.max).then_inc(s["mbase"], 1)

                    def ends_backward(g):
                        dve.wait_ge(s["mbase"], g.n + 1)
                        V.tensor_tensor_scan(flat(mrun[:, :, :])[:, ::-1], thru[0:1, n1:0:-1], mbase[:, ::-1], 0.0,
                                             ALU.mult, ALU.max).then_inc(s["mrun"], 1)

                    def ends_out(g):
                        dve.wait_ge(s["mrun"], g.n + 1)
                        V.tensor_tensor(cfirst[:, :, :], mrun[:, :, 0:GS], bsh(eq_row[0:1, slots(g)]), ALU.mult).then_inc(s["cfirst"], 1)
                        V.tensor_copy(clast[:, :, :], mrun[:, :, 1:GS + 1]).then_inc(s["clast"], 1)
                        V.tensor_tensor(drop[:, :], lmax[:, :, 0], mrun[:, :, 0], ALU.subtract).then_inc(s["drop"], 1)

                    def carry_over(g):
                        dve.wait_ge(s["drop"], g.n + 1)
                        V.tensor_copy(lmax[:, :, 0:1], mrun[:, :, GS:GS + 1]).then_inc(s["carry"], 1)

                    def spread_ends(g):
                        dve.wait_ge(s["cols_ps"], g.n + 1)
                        r = rel_r[:, g.slot, :]
                        V.tensor_scalar(from_first[:, :], r, r[:, 0:1], ps_cols[:, 0:1], ALU.is_equal, ALU.mult).then_inc(s["from_first"], 1)
                        V.tensor_scalar(from_last[:, :], r, r[:, P - 1:P], ps_cols[:, 1:2], ALU.is_equal, ALU.mult).then_inc(s["from_last"], 1)

                    def alpha_argument(g):
                        if not g.first:
                            dve.wait_ge(s["alpha"], g.n)
                        V.tensor_scalar(alpha_arg[:, :], ps_drop, first_ind[:, ds(g.n, 1)], None, ALU.mult).then_inc(s["alpha_arg"], 1)

                    def max_first(g):
                        dve.wait_ge(s["from_first"], g.n + 1)
                        V.tensor_tensor(rm1[:, :], rmax[:, :], from_first[:, :], ALU.max).then_inc(s["rm1"], 1)

                    def max_last(g):
                        dve.wait_ge(s["rm1"], g.n + 1)
                        dve.wait_ge(s["from_last"], g.n + 1)
                        V.tensor_tensor(mx[:, :], rm1[:, :], from_last[:, :], ALU.max).then_inc(s["mx"], 1)

                    def exponent(g):
                        dve.wait_ge(s["m_ps"], g.n + 1)
                        V.tensor_tensor(flat(arg[:, :, :]), flat(att[:, g.slot, :, :]), ps_m, ALU.subtract).then_inc(s["arg"], 1)

                    vh = vals[:, :, :].rearrange("p s (h c) -> p s h c", h=HEADS)

                    def weighted_rows(g):
                        dve.wait_ge(s["ex"], g.n + 1)
                        if not g.first:
                            dve.wait_ge(s["sum_ps"], g.n * len(BATCHES))
                        V.tensor_tensor(vh[:, :, :, 0:HD], gath[:, g.slot, :, 0:NODE_DIM].rearrange("p s (h c) -> p s h c", h=HEADS),
                                        ex[:, :, :].rearrange("p h s -> p s h").unsqueeze(3).broadcast_to((P, GS, HEADS, HD)), ALU.mult).then_inc(s["vals_h"], 1)

                    def last_edges(g):
                        dve.wait_ge(s["enm"], g.n + 1)
                        V.tensor_tensor(lastex[:, :, :], enm[:, :, :], bsh(last_s[:, slots(g)]), ALU.mult).then_inc(s["lastex"], 1)

                    def weights(g):
                        dve.wait_ge(s["lastex"], g.n + 1)
                        dve.wait_ge(s["vals_h"], g.n + 1)
                        V.tensor_tensor(vh[:, :, :, HD], ex[:, :, :].rearrange("p h s -> p s h"), lastex[:, :, :].rearrange("p h s -> p s h"),
                                        ALU.add).then_inc(s["vals"], 1)

                    def body(g, prev, nxt, second):
                        same_key(g)
                        run_max_forward(g)
                        run_max(g)
                        blocks = load_blocks(prev) if prev else None
                        left = list(range(GS)) if prev else []

                        def adds(n):
                            for _ in range(n):
                                if left:
                                    add(prev, blocks, left.pop(0))

                        if prev:
                            rescale(prev, blocks)
                        thru_flags(g)
                        adds(1)
                        end_values(g)
                        adds(1)
                        ends_forward(g)
                        adds(1)
                        ends_base(g)
                        adds(1)
                        ends_backward(g)
                        adds(1)
                        ends_out(g)
                        adds(2)
                        spread_ends(g)
                        alpha_argument(g)
                        max_first(g)
                        carry_over(g)
                        max_last(g)
                        adds(2)
                        exponent(g)
                        adds(3)
                        if nxt:
                            add_source(nxt)
                            adds(1)
                            add_target(nxt)
                            adds(1)
                            leaky(nxt)
                        adds(GS)
                        if second:
                            make_onehot(second)
                        last_edges(g)
                        weighted_rows(g)
                        weights(g)

                    def start(g, second):
                        for step in (make_onehot, add_source, add_target, leaky):
                            step(g)
                        make_onehot(second)

                    def finish(g):
                        blocks = load_blocks(g)
                        rescale(g, blocks)
                        for j in range(GS):
                            add(g, blocks, j)

                    iterations(dve, start, body, finish)

        with ExitStack() as stage:
            def ssem(name):
                return stage.enter_context(nc.semaphore(name))

            def ssb(name, shape, dt):
                return stage.enter_context(nc.sbuf_tensor(name, shape, dt))

            W = 2 * NODE_GROUP
            n_out = N_BLOCKS // W
            xo, yo = (t[:, 0:2 * W * NODE_DIM].rearrange("p (q w d) -> p q w d", q=2, w=W) for t in (gath_flat, oh_flat))
            den = ssb("den", [P, 2, W * HEADS], f32)
            s_x, s_out = [ssem(f"x_again{q}") for q in range(2)], [ssem(f"stored{q}") for q in range(2)]
            s_e, s_d, s_r, s_m, s_y = ssem("empty_nodes"), ssem("denominators"), ssem("reciprocals"), ssem("normalised"), ssem("results")
            x_g = x.rearrange("(g i p) d -> g p i d", i=W, p=P)
            out_g = out.rearrange("(g i p) d -> g p i d", i=W, p=P)
            with nc.Block() as block:
                @block.sync
                def _(sp):
                    for g in range(n_out):
                        if g >= 2:
                            sp.wait_ge(s_y, g - 1)
                        sp.dma_start(xo[:, g % 2, :, :], x_g[g, :, :, :]).then_inc(s_x[g % 2], 16)

                @block.scalar
                def _(act):
                    for g in range(n_out):
                        act.wait_ge(s_y, g + 1)
                        act.dma_start(out_g[g, :, :, :], yo[:, g % 2, :, :]).then_inc(s_out[g % 2], 16)
                    for q in range(2):
                        act.wait_ge(s_out[q], 16 * len(range(q, n_out, 2)))

                @block.vector
                def _(dve):
                    V = nc.vector
                    for g in range(n_out):
                        q = g % 2
                        a4 = acc_b[:, g * W:(g + 1) * W, :].rearrange("p b (h c) -> p (b h) c", h=HEADS)
                        V.tensor_scalar(den[:, 0, :], a4[:, :, HD], 0.0, None, ALU.is_equal).then_inc(s_e, 1)
                        dve.wait_ge(s_e, g + 1)
                        V.tensor_tensor(den[:, 1, :], a4[:, :, HD], den[:, 0, :], ALU.add).then_inc(s_d, 1)
                        dve.wait_ge(s_d, g + 1)
                        V.reciprocal(den[:, 0, :], den[:, 1, :]).then_inc(s_r, 1)
                        dve.wait_ge(s_r, g + 1)
                        if g >= 2:
                            dve.wait_ge(s_out[q], 16 * (g // 2))
                        y3 = yo[:, q, :, :].rearrange("p b (h c) -> p (b h) c", h=HEADS)
                        V.tensor_tensor(y3, a4[:, :, 0:HD], den[:, 0, :].unsqueeze(2).broadcast_to((P, W * HEADS, HD)), ALU.mult).then_inc(s_m, 1)
                        dve.wait_ge(s_m, g + 1)
                        dve.wait_ge(s_x[q], 16 * (g // 2 + 1))
                        V.tensor_tensor(yo[:, q, :, :], yo[:, q, :, :], xo[:, q, :, :], ALU.add).then_inc(s_y, 1)


def kernel(**inputs):
    import numpy as np
    import concourse.bacc as bacc
    from concourse.bass_utils import run_bass_kernel_spmd

    x = np.zeros((N_BLOCKS * P, NODE_DIM), np.float32)
    x[:N_NODES] = inputs["x"]
    src = np.zeros((NS * P,), np.int32)
    src[:N_EDGES] = inputs["src"]
    dst = np.full((NS * P + 2,), PAD_DST, np.int32)
    dst[1:N_EDGES + 1] = inputs["dst"]
    ea = np.zeros((N_TILES * P, EDGE_DIM), np.float32)
    ea[:N_EDGES] = inputs["edge_attr_64"]
    arrays = {"x_in": x, "src_in": src, "dst_in": dst, "edge_attr_in": ea,
              "w_node_in": np.ascontiguousarray(inputs["L0_gnn_W_node"]),
              "w_edge_in": np.ascontiguousarray(inputs["L0_gnn_W_edge"]),
              "a_in": np.ascontiguousarray(inputs["L0_gnn_a"])}
    nc = bacc.Bacc("TRN2", target_bir_lowering=False, num_devices=1)
    args = [nc.dram_tensor(n, v.shape, mybir.dt.from_np(v.dtype), kind="ExternalInput").ap() for n, v in arrays.items()]
    out = nc.dram_tensor("out_dram", (N_BLOCKS * P, NODE_DIM), mybir.dt.float32, kind="ExternalOutput").ap()
    gat_kernel(nc, *args, out)
    r = run_bass_kernel_spmd(nc, [arrays], core_ids=[0])
    return r.results[0]["out_dram"][:N_NODES]
```
